# Optimizing a Trainium2 kernel written in Bass

```python
import numpy as np
import jax
import jax.numpy as jnp

def _softmax(x, axis=-1):
    return jax.nn.softmax(x, axis=axis)

def _gelu(x):
    return jax.nn.gelu(x, approximate=True)

def _silu(x):
    return jax.nn.silu(x)

def _sigmoid(x):
    return jax.nn.sigmoid(x)

def _layernorm(x, axis=-1, eps=1e-05):
    m = jnp.mean(x, axis=axis, keepdims=True)
    v = jnp.var(x, axis=axis, keepdims=True)
    return (x - m) / jnp.sqrt(v + eps)

def _scatter_add(tgt, idx, src, axis=0):
    return tgt.at[idx].add(src)

def _segment_sum(src, seg, n):
    return jax.ops.segment_sum(src, seg, n)
kernel_name = 'mk_prb_d1_jaxref_r8_848171'

def setup_inputs(seed: int=0):
    np.random.seed(seed)
    _w = jnp.asarray

    def _L0_attn_setup():
        import jax, jax.numpy as jnp
        import numpy as np
        HIDDEN = 512
        HEAD_DIM = 128
        N_Q_HEADS = 32
        N_KV_HEADS = 8
        SLIDING_WINDOW = 128
        ROPE_THETA = 10000.0
        BATCH, SEQ = (1, 256)

        def _rope(t, pos):
            d = t.shape[-1]
            half = d // 2
            inv_freq = ROPE_THETA ** (-jnp.arange(half, dtype=jnp.float32) / half)
            ang = pos[:, None].astype(jnp.float32) * inv_freq[None, :]
            cos = jnp.cos(ang)[None, :, None, :]
            sin = jnp.sin(ang)[None, :, None, :]
            t1, t2 = (t[..., :half], t[..., half:])
            return jnp.concatenate([t1 * cos - t2 * sin, t1 * sin + t2 * cos], axis=-1)
        key = jax.random.key(seed)
        ks = jax.random.split(key, 5)
        w_scale = HIDDEN ** (-0.5)
        return {'x': jax.random.normal(ks[0], (BATCH, SEQ, HIDDEN), jnp.float32), 'wq': jax.random.normal(ks[1], (HIDDEN, N_Q_HEADS * HEAD_DIM), jnp.float32) * w_scale, 'wk': jax.random.normal(ks[2], (HIDDEN, N_KV_HEADS * HEAD_DIM), jnp.float32) * w_scale, 'wv': jax.random.normal(ks[3], (HIDDEN, N_KV_HEADS * HEAD_DIM), jnp.float32) * w_scale, 'wo': jax.random.normal(ks[4], (N_Q_HEADS * HEAD_DIM, HIDDEN), jnp.float32) * w_scale}
    _L0_attn_in = _L0_attn_setup()

    def _L0_ffn_setup():
        import jax, jax.numpy as jnp
        import numpy as np
        H, FF = (512, 1792)
        B, S = (4, 256)
        key = jax.random.key(seed)
        ks = jax.random.split(key, 7)
        x = jax.random.normal(ks[0], (B, S, H), dtype=jnp.float32)
        gate_t = jax.random.randint(ks[1], (FF, H), -1, 2, dtype=jnp.int32)
        up_t = jax.random.randint(ks[2], (FF, H), -1, 2, dtype=jnp.int32)
        down_t = jax.random.randint(ks[3], (H, FF), -1, 2, dtype=jnp.int32)
        gate_s = jax.random.uniform(ks[4], (FF,), jnp.float32, 0.01, 0.1)
        up_s = jax.random.uniform(ks[5], (FF,), jnp.float32, 0.01, 0.1)
        down_s = jax.random.uniform(ks[6], (H,), jnp.float32, 0.01, 0.1)
        return {'x': x, 'gate_t': gate_t, 'up_t': up_t, 'down_t': down_t, 'gate_s': gate_s, 'up_s': up_s, 'down_s': down_s}
    _L0_ffn_in = _L0_ffn_setup()
    _d = {'L0_attn_x': _L0_attn_in['x'], 'L0_attn_wq': _L0_attn_in['wq'], 'L0_attn_wk': _L0_attn_in['wk'], 'L0_attn_wv': _L0_attn_in['wv'], 'L0_attn_wo': _L0_attn_in['wo'], 'L0_ffn_gate_t': _L0_ffn_in['gate_t'], 'L0_ffn_up_t': _L0_ffn_in['up_t'], 'L0_ffn_down_t': _L0_ffn_in['down_t'], 'L0_ffn_gate_s': _L0_ffn_in['gate_s'], 'L0_ffn_up_s': _L0_ffn_in['up_s'], 'L0_ffn_down_s': _L0_ffn_in['down_s']}
    _x0 = _d['L0_attn_x']
    _d['L0_attn_x'] = jax.random.normal(jax.random.fold_in(jax.random.key(seed), 1), (8, 256, 512), dtype=_x0.dtype)
    del _x0
    return _d

def reference(L0_attn_x, L0_attn_wq, L0_attn_wk, L0_attn_wv, L0_attn_wo, L0_ffn_gate_t, L0_ffn_up_t, L0_ffn_down_t, L0_ffn_gate_s, L0_ffn_up_s, L0_ffn_down_s):

    def _L0_attn_ref(x, wq, wk, wv, wo):
        import jax, jax.numpy as jnp
        import numpy as np
        HIDDEN = 512
        HEAD_DIM = 128
        N_Q_HEADS = 32
        N_KV_HEADS = 8
        SLIDING_WINDOW = 128
        ROPE_THETA = 10000.0
        BATCH, SEQ = (1, 256)

        def _rope(t, pos):
            d = t.shape[-1]
            half = d // 2
            inv_freq = ROPE_THETA ** (-jnp.arange(half, dtype=jnp.float32) / half)
            ang = pos[:, None].astype(jnp.float32) * inv_freq[None, :]
            cos = jnp.cos(ang)[None, :, None, :]
            sin = jnp.sin(ang)[None, :, None, :]
            t1, t2 = (t[..., :half], t[..., half:])
            return jnp.concatenate([t1 * cos - t2 * sin, t1 * sin + t2 * cos], axis=-1)
        B, S, _ = x.shape
        G = N_Q_HEADS // N_KV_HEADS
        sm_scale = HEAD_DIM ** (-0.5)
        q = (x @ wq).reshape(B, S, N_Q_HEADS, HEAD_DIM)
        k = (x @ wk).reshape(B, S, N_KV_HEADS, HEAD_DIM)
        v = (x @ wv).reshape(B, S, N_KV_HEADS, HEAD_DIM)
        pos = jnp.arange(S)
        q = _rope(q, pos)
        k = _rope(k, pos)
        qg = q.reshape(B, S, N_KV_HEADS, G, HEAD_DIM)
        scores = jnp.einsum('bqhgd,bshd->bhgqs', qg, k) * sm_scale
        i = pos[:, None]
        j = pos[None, :]
        allowed = (j <= i) & (j > i - SLIDING_WINDOW)
        neg = jnp.finfo(scores.dtype).min
        scores = jnp.where(allowed[None, None, None], scores, neg)
        attn = jax.nn.softmax(scores, axis=-1)
        out = jnp.einsum('bhgqs,bshd->bqhgd', attn, v).reshape(B, S, N_Q_HEADS * HEAD_DIM)
        return out @ wo

    def _L0_ffn_ref(x, gate_t, up_t, down_t, gate_s, up_s, down_s):
        import jax, jax.numpy as jnp
        import numpy as np
        H, FF = (512, 1792)
        B, S = (4, 256)
        Bb, Ss, Hh = x.shape
        x_flat = x.reshape(Bb * Ss, Hh)
        gate_w = gate_t.astype(jnp.float32) * gate_s[:, None]
        up_w = up_t.astype(jnp.float32) * up_s[:, None]
        down_w = down_t.astype(jnp.float32) * down_s[:, None]
        gate_out = x_flat @ gate_w.T
        up_out = x_flat @ up_w.T
        hidden = jax.nn.silu(gate_out) * up_out
        out_flat = hidden @ down_w.T
        return out_flat.reshape(Bb, Ss, -1)
    x = L0_attn_x
    xn = _layernorm(x, axis=-1)
    x = x + _L0_attn_ref(xn, L0_attn_wq, L0_attn_wk, L0_attn_wv, L0_attn_wo) + _L0_ffn_ref(xn, L0_ffn_gate_t, L0_ffn_up_t, L0_ffn_down_t, L0_ffn_gate_s, L0_ffn_up_s, L0_ffn_down_s)
    return x

_drawn_inputs = setup_inputs


def setup_inputs(seed=0):
    import zlib

    import numpy as np

    out = dict(_drawn_inputs(seed))
    spreads = {}
    factors = {}
    for name, (base, spread) in spreads.items():
        noise = np.random.default_rng([zlib.crc32(name.encode()), seed]).standard_normal(out[name].shape)
        drawn = base * np.exp(spread * noise) if base else spread * noise
        out[name] = jnp.asarray(drawn.astype(out[name].dtype))
    for name, factor in factors.items():
        out[name] = (out[name] * factor).astype(out[name].dtype)
    return out
```

```python
from contextlib import ExitStack

import concourse.bass as bass
import numpy as np
from concourse import mybir

F32 = mybir.dt.float32
F32R = mybir.dt.float32r
I32 = mybir.dt.int32
BF16 = mybir.dt.bfloat16
ACT = mybir.ActivationFunctionType
ALU = mybir.AluOpType
AX = mybir.AxisListType

P = 128
BATCH, SEQ, HID = 8, 256, 512
TOKENS = BATCH * SEQ
FF = 1792
Q_HEADS, KV_HEADS, DH = 32, 8, 128
HALF = DH // 2
WINDOW = 128
THETA = 10000.0
EPS = 1e-5
SM_SCALE = DH ** -0.5
MASKED = -3.0e38
BIGGEST = 3.4e38

KB = HID // P
CHUNK = 512
CHUNKS = TOKENS // CHUNK
TB = CHUNK // P
G = Q_HEADS // KV_HEADS
FBLOCKS = FF // P
PAIRS = FBLOCKS // 2
TILES = TOKENS // P

K_TILE, Q_TILE, V_TILE, O_TILE = 0, 1, 1 + G, 2 + G
IN_TILES, W_TILES = 2 + G, 2 + 2 * G
RAW = 5
F_TILES = 6


def rope_tables():
    inv_freq = np.float32(THETA) ** (-np.arange(HALF, dtype=np.float32) / np.float32(HALF))
    angle = np.arange(SEQ, dtype=np.float32)[None, :] * inv_freq.astype(np.float32)[:, None]
    cos, sin = np.cos(angle), np.sin(angle)
    return np.concatenate([np.concatenate([cos, cos]), np.concatenate([-sin, sin])], axis=1).astype(np.float32)


def score_masks():
    i, j = np.arange(P)[:, None], np.arange(P)[None, :]
    causal = np.where(j <= i, 0.0, MASKED)
    window = np.where(j > i + P - WINDOW, 0.0, MASKED)
    return np.concatenate([causal, window, causal], axis=1).astype(np.float32)


def block_kernel(nc, x, wq, wk, wv, wo, gate, up, down, gate_s, up_s, down_s, rope, masks, ident, out):
    with ExitStack() as ctx:
        def sem(name):
            return ctx.enter_context(nc.semaphore(name))

        def tensors(stack, **shapes):
            return [stack.enter_context(nc.sbuf_tensor(n, s, d)) for n, (s, d) in shapes.items()]

        xt_hi, xt_lo, acc, rope_sb, mask_sb, ident_sb, gs_sb, us_sb, ds_sb = tensors(
            ctx, xt_hi=([P, KB, TOKENS], F32R), xt_lo=([P, KB, TOKENS], F32R),
            acc=([P, TILES, HID], F32), rope_sb=([P, 2, SEQ], F32), mask_sb=([P, 3 * P], F32),
            ident_sb=([P, P], F32), gs_sb=([P, FBLOCKS], F32), us_sb=([P, FBLOCKS], F32),
            ds_sb=([P, HID], F32))
        with ExitStack() as ff:
            (fw_hi, fw_lo, h_hi, h_lo, fraw, gated, magnitudes, stats, moments, var_eps, power, rstd, peaks,
             flags, xn, h32) = tensors(
                ff, fw_hi=([P, F_TILES, 512], F32R), fw_lo=([P, F_TILES, 512], F32R),
                h_hi=([P, 2, TOKENS], F32R), h_lo=([P, 2, TOKENS], F32R),
                fraw=([P, F_TILES, 512], I32), gated=([P, 2, CHUNK], F32),
                magnitudes=([P, 4, 512], BF16), stats=([P, TILES, 6], F32),
                moments=([P, TILES, 2], F32), var_eps=([P, TILES], F32), power=([P, TB], F32),
                rstd=([P, TILES], F32), peaks=([P, 2], F32), flags=([P, 2], F32),
                xn=([P, 2, TB, HID], F32), h32=([P, 2, CHUNK], F32))
        (aw_hi, aw_lo, q_sb, k_sb, swap, vt_sb, v_hi, v_lo, s_late, s_early, pt_hi, pt_lo, at_hi, at_lo,
         negmax, sums, rsums, araw) = tensors(
            ctx, aw_hi=([P, W_TILES, 512], F32R), aw_lo=([P, W_TILES, 512], F32R),
            q_sb=([P, G, CHUNK], F32), k_sb=([P, 2, CHUNK], F32), swap=([P, 2, CHUNK], F32),
            vt_sb=([P, CHUNK], F32), v_hi=([P, TB, DH], F32R), v_lo=([P, TB, DH], F32R),
            s_late=([P, 2, G, 2 * P], F32), s_early=([P, 2, G, P], F32),
            pt_hi=([P, 3, G * P], F32R), pt_lo=([P, 3, G * P], F32R),
            at_hi=([P, 2, G * P], F32R), at_lo=([P, 2, G * P], F32R),
            negmax=([P, 2, 2 * G], F32), sums=([P, 2, 2 * G], F32), rsums=([P, 2, 2 * G], F32),
            araw=([P, RAW, 512], F32))
        scaled = xn[:].rearrange("p a t h -> p (a t) h")
        SCALED = 2 * TB
        bank = [ctx.enter_context(nc.psum_tensor(f"bank{i}", [P, 512], F32)) for i in range(8)]

        x_loaded = [[sem(f"x_loaded{c}_{t}") for t in range(TB)] for c in range(CHUNKS)]
        ident_loaded, scales_loaded, tables_loaded = sem("ident_loaded"), sem("scales_loaded"), sem("tables_loaded")
        stats_done, moments_done, eps_added = sem("stats_done"), sem("moments_done"), sem("eps_added")
        power_set, rstd_done, xn_done = sem("power_set"), sem("rstd_done"), sem("xn_done")
        xt_ready, xt_hi_done, xt_lo_done = sem("xt_ready"), sem("xt_hi_done"), sem("xt_lo_done")
        fraw_loaded = [sem(f"fraw_loaded{i}") for i in range(F_TILES)]
        fw_hi_done, fw_lo_done = sem("fw_hi_done"), sem("fw_lo_done")
        peak_done, flag_done = sem("peak_done"), sem("flag_done")
        gate_ready, up_ready, silu_done, h32_done = sem("gate_ready"), sem("up_ready"), sem("silu_done"), sem("h32_done")
        h_hi_done, h_lo_done = sem("h_hi_done"), sem("h_lo_done")
        down_ready, down_scaled, ff_added = sem("down_ready"), sem("down_scaled"), sem("ff_added")
        araw_loaded = [sem(f"araw_loaded{i}") for i in range(RAW)]
        aw_hi_done, aw_lo_done = sem("aw_hi_done"), sem("aw_lo_done")
        proj_ready, swapped, cos_done, sin_done, qk_done = (
            sem("proj_ready"), sem("swapped"), sem("cos_done"), sem("sin_done"), sem("qk_done"))
        vt_done, v_ready, v_hi_done, v_done = sem("vt_done"), sem("v_ready"), sem("v_hi_done"), sem("v_done")
        scores_ready, scores_used, exp_done = sem("scores_ready"), sem("scores_used"), sem("exp_done")
        rsums_done, probs_done = sem("rsums_done"), sem("probs_done")
        pt_ready, pt_hi_done, pt_done = sem("pt_ready"), sem("pt_hi_done"), sem("pt_done")
        at_ready, at_hi_done, at_done = sem("at_ready"), sem("at_hi_done"), sem("at_done")
        wo_ready, wo_added, stored = sem("wo_ready"), sem("wo_added"), sem("stored")

        def in_pass(r, per_pass, item, before=0):
            return r * per_pass + (item + 1 + before)

        def in_step(g, c, per_step, item, before=0):
            return g * (CHUNKS * per_step) + (c * per_step + item + 1 + before)

        def held(engine, count):
            return count if isinstance(count, int) else engine.to_reg(count)

        def tokens(c):
            return slice(c * CHUNK, (c + 1) * CHUNK)

        def f32(ap):
            return ap.bitcast(F32)

        def weight_block(w, tile, kb):
            return w[:, tile, kb * P:(kb + 1) * P]

        GU = 2 * CHUNKS
        GATE_UP, DOWN = 0, 1
        PT_BANK = (5, 6)
        AT_BANK = 7

        block = ctx.enter_context(nc.Block())

        @block.sync
        def _(sp):
            x_v = x.rearrange("(c t p) h -> c p t h", c=CHUNKS, p=P)
            out_v = out.rearrange("(c t p) h -> c p t h", c=CHUNKS, p=P)
            def load_x(c):
                for t in range(TB):
                    sp.dma_start(acc[:, c * TB + t, :], x_v[c][:, t, :]).then_inc(x_loaded[c][t], 16)

            def load_ff(r, tile):
                src = (gate, up, gate, up, down, down)[tile]
                f = r * 2 + (0, 0, 1, 1, 0, 1)[tile]
                sp.dma_start(fraw[:, tile, :], src[f]).then_inc(fraw_loaded[tile], 16)

            load_x(0)
            sp.dma_start(ident_sb[:], ident).then_inc(ident_loaded, 16)
            for tile in (0, 1):
                load_ff(0, tile)
            load_x(1)
            for tile in range(2, F_TILES):
                load_ff(0, tile)
            for c in range(2, CHUNKS):
                load_x(c)
            for dst, src in ((gs_sb, gate_s), (us_sb, up_s)):
                sp.dma_start(dst[:], src).then_inc(scales_loaded, 16)
            sp.dma_start(ds_sb[:], down_s.partition_broadcast(P)).then_inc(scales_loaded, 16)
            sp.dma_start(rope_sb[:].rearrange("p a s -> p (a s)"), rope).then_inc(tables_loaded, 16)
            sp.dma_start(mask_sb[:], masks).then_inc(tables_loaded, 16)
            with sp.Fori(0, PAIRS - 1) as r:
                for tile in range(F_TILES):
                    sp.wait_ge(fw_lo_done, in_pass(r, F_TILES, tile))
                    load_ff(r + 1, tile)

            def load_attention(g, tile):
                slot = tile % RAW
                if tile == K_TILE:
                    src = wk[g]
                elif tile < V_TILE:
                    src = wq[g * G + (tile - Q_TILE)]
                elif tile == V_TILE:
                    src = wv[g]
                else:
                    src = wo[g * G + (tile - O_TILE)]
                sp.dma_start(araw[:, slot, :], src).then_inc(araw_loaded[slot], 16)

            sp.wait_ge(h_lo_done, GU * (PAIRS + 1))
            for tile in range(RAW):
                load_attention(0, tile)
            for tile in range(RAW, W_TILES):
                sp.wait_ge(aw_lo_done, tile - RAW + 1)
                load_attention(0, tile)
            with sp.Fori(0, KV_HEADS - 1) as g:
                for tile in range(W_TILES):
                    sp.wait_ge(aw_lo_done, g * W_TILES + (W_TILES + tile - RAW + 1))
                    load_attention(g + 1, tile)

            for c in range(CHUNKS):
                sp.wait_ge(wo_added, in_step(KV_HEADS - 1, c, TB, TB - 1, TB))
                sp.dma_start(out_v[c], acc[:, c * TB:(c + 1) * TB, :]).then_inc(stored, 16)
            sp.wait_ge(stored, 16 * CHUNKS)

        @block.tensor
        def _(pe):
            def product(dst, w_hi, w_lo, x_hi, x_lo, first, last, w_lo_too=True, x_lo_too=True):
                passes = [(w_hi, x_hi)] + [(w_hi, x_lo)] * x_lo_too + [(w_lo, x_hi)] * w_lo_too
                for n, (w, v) in enumerate(passes):
                    mm = nc.tensor.matmul(dst, w, v, start=first and n == 0,
                                          stop=last and n == len(passes) - 1)
                return mm

            def transpose_rows(c):
                pe.wait_ge(xn_done, TB * (c + 1))
                for kb in range(KB):
                    n = c * KB + kb
                    if c > 0:
                        pe.wait_ge(xt_lo_done, n - KB + 1)
                    for t in range(TB):
                        last = nc.tensor.transpose(bank[4 + kb][:, t * P:(t + 1) * P],
                                                   xn[:, c % 2, t, kb * P:(kb + 1) * P], ident_sb[:])
                    last.then_inc(xt_ready, 1)

            def gate_or_up(r, f, c, which, with_lo):
                n = f * CHUNKS + c
                ready, free = ((gate_ready, silu_done), (up_ready, h32_done))[which]
                if c == 0:
                    pe.wait_ge(fw_lo_done, in_pass(r, F_TILES, 2 * f + which))
                pe.wait_ge(free, in_pass(r, GU, n - 2, GU))
                for kb in range(KB):
                    last = product(bank[2 * which + n % 2][:], weight_block(fw_hi, 2 * f + which, kb),
                                   weight_block(fw_lo, 2 * f + which, kb), xt_hi[:, kb, tokens(c)],
                                   xt_lo[:, kb, tokens(c)], kb == 0, kb == KB - 1, w_lo_too=with_lo)
                last.then_inc(ready, 1)

            def gates_and_ups(r, blocks, with_lo):
                for f in blocks:
                    for c in range(CHUNKS):
                        for which in range(2):
                            gate_or_up(r, f, c, which, with_lo)

            def downs(r, with_lo):
                for m in range(TILES):
                    c = m // TB
                    if m % TB == 0:
                        pe.wait_ge(h_lo_done, in_pass(r, GU, CHUNKS + c, GU))
                    pe.wait_ge(down_scaled, in_pass(r, TILES, m - 4, TILES))
                    rows = slice(m * P, (m + 1) * P)
                    for f in range(2):
                        last = product(bank[4 + m % 4][:], h_hi[:, f, rows], h_lo[:, f, rows],
                                       fw_hi[:, 4 + f, :], fw_lo[:, 4 + f, :], f == 0, f == 1,
                                       x_lo_too=with_lo)
                    last.then_inc(down_ready, 1)

            def by_flag(r, which, work):
                known = held(pe, in_pass(r, 2, 0 if which == GATE_UP else 1))
                pe.wait_ge(flag_done, 1)
                pe.wait_ge(flag_done, known)
                biggest_lo = pe.value_load(flags[0:1, which:which + 1].bitcast(I32))
                with pe.If_ne(pe.to_reg(biggest_lo), 0):
                    work(True)
                with pe.Else():
                    work(False)

            def ff_pass(r, blocks):
                by_flag(r, GATE_UP, lambda with_lo: gates_and_ups(r, blocks, with_lo))
                by_flag(r, DOWN, lambda with_lo: downs(r, with_lo))

            pe.wait_ge(ident_loaded, 16)
            transpose_rows(0)
            for c in range(CHUNKS):
                pe.wait_ge(xt_lo_done, KB * (c + 1))
                gate_or_up(0, 0, c, 0, True)
                if c + 1 < CHUNKS:
                    transpose_rows(c + 1)
                gate_or_up(0, 0, c, 1, True)
            ff_pass(0, (1,))
            with pe.Fori(1, PAIRS) as r:
                ff_pass(r, (0, 1))

            pe.wait_ge(down_scaled, TILES * (PAIRS + 1))

            def project(g, c, j):
                if c == 0:
                    pe.wait_ge(aw_lo_done, g * W_TILES + (j + 1))
                if j >= 2:
                    pe.wait_ge(cos_done, in_step(g, c, 1 + G, j - 2))
                for kb in range(KB):
                    last = product(bank[j % 2][:], weight_block(aw_hi, j, kb), weight_block(aw_lo, j, kb),
                                   xt_hi[:, kb, tokens(c)], xt_lo[:, kb, tokens(c)], kb == 0, kb == KB - 1)
                last.then_inc(proj_ready, 1)

            def project_next(g, c, j):
                if j < 2:
                    pe.wait_ge(wo_added, in_step(g, c - 1, TB, 2 + j, TB))
                if c + 1 < CHUNKS:
                    project(g, c + 1, j)
                else:
                    project(g + 1, 0, j)

            def transpose_v():
                for t in range(TB):
                    last = nc.tensor.transpose(bank[AT_BANK][:, t * DH:(t + 1) * DH],
                                               vt_sb[:, t * P:(t + 1) * P], ident_sb[:])
                last.then_inc(v_ready, 1)

            def scores(g, c, b):
                if b == 0:
                    pe.wait_ge(qk_done, in_step(g, c, 1 + G, G))
                early, late = b * SEQ, b * SEQ + P
                keys = k_sb[:, c % 2, b * SEQ:(b + 1) * SEQ]
                for pair in range(G // 2):
                    pe.wait_ge(scores_used, in_step(g, c, 6, 3 * b + pair - 3, 6))
                    for h in (2 * pair, 2 * pair + 1):
                        last = nc.tensor.matmul(bank[2 + pair][:, (h % 2) * SEQ:(h % 2 + 1) * SEQ],
                                                q_sb[:, h, late:late + P], keys, start=True, stop=True)
                    last.then_inc(scores_ready, 1)
                pe.wait_ge(scores_used, in_step(g, c, 6, 3 * b - 1, 6))
                for h in range(G):
                    last = nc.tensor.matmul(bank[4][:, h * P:(h + 1) * P], q_sb[:, h, early:early + P],
                                            keys[:, 0:P], start=True, stop=True)
                last.then_inc(scores_ready, 1)

            def transpose_probs(g, c, b, i):
                n = 3 * b + i
                if i < 2:
                    pe.wait_ge(probs_done, in_step(g, c, 4, 2 * b + i))
                pe.wait_ge(pt_done, in_step(g, c, 6, n - 2, 6))
                for h in range(G):
                    src = s_early[:, b, h, :] if i == 0 else s_late[:, b, h, (i - 1) * P:i * P]
                    last = nc.tensor.transpose(bank[PT_BANK[n % 2]][:, h * P:(h + 1) * P], src, ident_sb[:])
                last.then_inc(pt_ready, 1)

            def attend(g, c, b, late):
                n = 2 * b + late
                pe.wait_ge(pt_done, in_step(g, c, 6, 3 * b + 2 * late))
                if n == 0:
                    pe.wait_ge(v_done, in_step(g, c, 1, 0))
                else:
                    pe.wait_ge(at_done, in_step(g, c, 4, n - 1))
                tiles = ((1, 2 * b), (2, 2 * b + 1)) if late else ((0, 2 * b),)
                for k, (i, t) in enumerate(tiles):
                    last = product(bank[AT_BANK][:], v_hi[:, t, :], v_lo[:, t, :], pt_hi[:, i, :],
                                   pt_lo[:, i, :], k == 0, k == len(tiles) - 1)
                last.then_inc(at_ready, 1)

            def output(g, c, b, late, has_next):
                n = 2 * b + late
                pe.wait_ge(at_done, in_step(g, c, 4, n))
                if n == 0 and c == 0:
                    pe.wait_ge(aw_lo_done, g * W_TILES + W_TILES)
                if n >= 2:
                    pe.wait_ge(wo_added, in_step(g, c, TB, n - 2, TB))
                elif not has_next:
                    pe.wait_ge(wo_added, in_step(g, c - 1, TB, n + 2, TB))
                elif n == 0:
                    pe.wait_ge(cos_done, in_step(g, c + 1, 1 + G, G))
                else:
                    pe.wait_ge(vt_done, in_step(g, c + 1, 1, 0))
                for h in range(G):
                    last = product(bank[n % 2][:], at_hi[:, late, h * P:(h + 1) * P],
                                   at_lo[:, late, h * P:(h + 1) * P], aw_hi[:, O_TILE + h, :],
                                   aw_lo[:, O_TILE + h, :], h == 0, h == G - 1)
                last.then_inc(wo_ready, 1)

            def step(g, c, has_next):
                scores(g, c, 0)
                if has_next:
                    project_next(g, c, K_TILE)
                scores(g, c, 1)
                if has_next:
                    for h in range(G - 1):
                        project_next(g, c, Q_TILE + h)
                transpose_probs(g, c, 0, 0)
                transpose_probs(g, c, 0, 1)
                if has_next:
                    project_next(g, c, Q_TILE + G - 1)
                transpose_probs(g, c, 0, 2)
                attend(g, c, 0, 0)
                if has_next:
                    project_next(g, c, V_TILE)
                transpose_probs(g, c, 1, 0)
                attend(g, c, 0, 1)
                transpose_probs(g, c, 1, 1)
                transpose_probs(g, c, 1, 2)
                output(g, c, 0, 0, has_next)
                attend(g, c, 1, 0)
                output(g, c, 0, 1, has_next)
                attend(g, c, 1, 1)
                output(g, c, 1, 0, has_next)
                if has_next:
                    pe.wait_ge(vt_done, in_step(g, c + 1, 1, 0))
                    pe.wait_ge(at_done, in_step(g, c, 4, 3))
                    transpose_v()
                output(g, c, 1, 1, has_next)

            for j in range(IN_TILES):
                project(0, 0, j)
            pe.wait_ge(vt_done, 1)
            transpose_v()
            with pe.Fori(0, KV_HEADS - 1) as g:
                for c in range(CHUNKS):
                    step(g, c, True)
            for c in range(CHUNKS):
                step(KV_HEADS - 1, c, c < CHUNKS - 1)

        @block.scalar
        def _(act):
            def xt_high(c):
                for kb in range(KB):
                    act.wait_ge(xt_ready, c * KB + kb + 1)
                    nc.scalar.activation(xt_hi[:, kb, tokens(c)], bank[4 + kb][:],
                                         ACT.Copy).then_inc(xt_hi_done, 1)

            def split_ff(r, tile):
                act.wait_ge(fraw_loaded[tile], r * 16 + 16)
                nc.scalar.activation(fw_hi[:, tile, :], fraw[:, tile, :], ACT.Copy).then_inc(fw_hi_done, 1)

            def h_high(r, n):
                act.wait_ge(h32_done, in_pass(r, GU, n, GU))
                nc.scalar.activation(h_hi[:, n // CHUNKS, tokens(n % CHUNKS)], h32[:, n % 2, :],
                                     ACT.Copy).then_inc(h_hi_done, 1)

            def find_peak(r, which):
                tiles = slice(0, 4) if which == GATE_UP else slice(4, 6)
                act.wait_ge(fw_lo_done, in_pass(r, F_TILES, tiles.stop - 1))
                nc.scalar.activation(magnitudes[:, 0:tiles.stop - tiles.start, :], f32(fw_lo[:, tiles, :]),
                                     ACT.Abs, accum_out=peaks[:, which:which + 1]).then_inc(peak_done, 1)

            def ff_pass(r, has_next, with_rows=False):
                for n in range(GU):
                    slot_read = held(act, in_pass(r, GU, n - 2, GU))
                    ready = held(act, in_pass(r, GU, n))
                    act.wait_ge(scales_loaded, 48)
                    act.wait_ge(gate_ready, ready)
                    act.wait_ge(h32_done, slot_read)
                    f = n // CHUNKS
                    nc.scalar.activation(gated[:, n % 2, :], bank[n % 2][:], ACT.Silu,
                                         scale=gs_sb[:, bass.ds(r * 2 + f, 1)]).then_inc(silu_done, 1)
                    if with_rows and n + 1 < CHUNKS:
                        xt_high(n + 1)
                    if n > 0:
                        h_high(r, n - 1)
                    if with_rows and n == CHUNKS - 1:
                        find_peak(0, GATE_UP)
                    if n == CHUNKS + 1:
                        find_peak(r, DOWN)
                    if n == 0:
                        for tile in (4, 5):
                            split_ff(r, tile)
                    if n == CHUNKS and has_next:
                        act.wait_ge(up_ready, in_pass(r, GU, n - 1))
                        for tile in (0, 1):
                            split_ff(r + 1, tile)
                h_high(r, GU - 1)
                if has_next:
                    act.wait_ge(up_ready, in_pass(r, GU, GU - 1))
                    for tile in (2, 3):
                        split_ff(r + 1, tile)
                    find_peak(r + 1, GATE_UP)

            for tile in (0, 1):
                split_ff(0, tile)
            xt_high(0)
            for tile in (2, 3):
                split_ff(0, tile)
            ff_pass(0, True, with_rows=True)
            with act.Fori(1, PAIRS - 1) as r:
                ff_pass(r, True)
            ff_pass(PAIRS - 1, False)

            def swap_halves(g, c, j):
                n = (1 + G) * c + j
                act.wait_ge(proj_ready, in_step(g, c, IN_TILES, j))
                if not (isinstance(g, int) and g == 0 and n < 2):
                    act.wait_ge(qk_done, in_step(g, c, 1 + G, j - 2))
                nc.scalar.activation(swap[0:HALF, n % 2, :], bank[j % 2][HALF:P, :], ACT.Copy)
                nc.scalar.activation(swap[HALF:P, n % 2, :], bank[j % 2][0:HALF, :],
                                     ACT.Copy).then_inc(swapped, 1)

            def copy_vt(g, c):
                act.wait_ge(proj_ready, in_step(g, c, IN_TILES, V_TILE))
                nc.scalar.activation(vt_sb[:], bank[V_TILE % 2][:], ACT.Copy).then_inc(vt_done, 1)

            def v_high(g, c):
                act.wait_ge(v_ready, in_step(g, c, 1, 0))
                nc.scalar.activation(v_hi[:].rearrange("p t d -> p (t d)"), bank[AT_BANK][:],
                                     ACT.Copy).then_inc(v_hi_done, 1)

            def exponentials(g, c, b, which):
                act.wait_ge(scores_used, in_step(g, c, 6, 3 * b + which, 6))
                heads = (0, 1, 2, 3) if which == 2 else (2 * which, 2 * which + 1)
                for h in heads:
                    s = s_early[:, b, h, :] if which == 2 else s_late[:, b, h, :]
                    col = h + (G if which == 2 else 0)
                    last = nc.scalar.activation(s, s, ACT.Exp, scale=-1.0, bias=negmax[:, b, col:col + 1],
                                                accum_out=sums[:, b, col:col + 1])
                last.then_inc(exp_done, 1)

            def pt_high(g, c, b, i):
                n = 3 * b + i
                act.wait_ge(pt_ready, in_step(g, c, 6, n))
                if b == 1:
                    act.wait_ge(at_ready, in_step(g, c, 4, 0 if i == 0 else 1))
                nc.scalar.activation(pt_hi[:, i, :], bank[PT_BANK[n % 2]][:], ACT.Copy).then_inc(pt_hi_done, 1)

            def at_high(g, c, b, late):
                n = 2 * b + late
                act.wait_ge(at_ready, in_step(g, c, 4, n))
                if b == 1:
                    act.wait_ge(wo_ready, in_step(g, c, TB, late))
                nc.scalar.activation(at_hi[:, late, :], bank[AT_BANK][:], ACT.Copy).then_inc(at_hi_done, 1)

            def step(g, c, has_next):
                ng, nxt = (g, c + 1) if c + 1 < CHUNKS else (g + 1, 0)
                for which in range(3):
                    exponentials(g, c, 0, which)
                if has_next:
                    swap_halves(ng, nxt, K_TILE)
                exponentials(g, c, 1, 0)
                exponentials(g, c, 1, 1)
                if has_next:
                    swap_halves(ng, nxt, Q_TILE)
                exponentials(g, c, 1, 2)
                if has_next:
                    swap_halves(ng, nxt, Q_TILE + 1)
                    swap_halves(ng, nxt, Q_TILE + 2)
                pt_high(g, c, 0, 0)
                pt_high(g, c, 0, 1)
                if has_next:
                    swap_halves(ng, nxt, Q_TILE + 3)
                pt_high(g, c, 0, 2)
                at_high(g, c, 0, 0)
                if has_next:
                    copy_vt(ng, nxt)
                pt_high(g, c, 1, 0)
                at_high(g, c, 0, 1)
                pt_high(g, c, 1, 1)
                pt_high(g, c, 1, 2)
                at_high(g, c, 1, 0)
                at_high(g, c, 1, 1)
                if has_next:
                    v_high(ng, nxt)

            for j in range(1 + G):
                swap_halves(0, 0, j)
            copy_vt(0, 0)
            v_high(0, 0)
            with act.Fori(0, KV_HEADS - 1) as g:
                for c in range(CHUNKS):
                    step(g, c, True)
            for c in range(CHUNKS):
                step(KV_HEADS - 1, c, c < CHUNKS - 1)

        @block.vector
        def _(dve):
            for s, n in ((silu_done, GU), (h32_done, GU), (h_lo_done, GU), (down_scaled, TILES),
                         (ff_added, TILES), (scores_used, 6), (pt_done, 6), (wo_added, TB)):
                dve.sem_inc(s, n)

            def statistics(c):
                for t in range(TB):
                    dve.wait_ge(x_loaded[c][t], 16)
                    last = nc.vector.bn_stats(stats[:, c * TB + t, :], acc[:, c * TB + t, :])
                last.then_inc(stats_done, 1)
                dve.wait_ge(stats_done, c + 1)
                for t in range(c * TB, (c + 1) * TB):
                    last = nc.vector.bn_aggr(moments[:, t, :], stats[:, t, :])
                last.then_inc(moments_done, 1)
                dve.wait_ge(moments_done, c + 1)
                cols = slice(c * TB, (c + 1) * TB)
                nc.vector.tensor_scalar(var_eps[:, cols], moments[:, cols, 1], EPS, None,
                                        ALU.add).then_inc(eps_added, 1)

            def normalise(c):
                dve.wait_ge(rstd_done, c + 1)
                if c >= 2:
                    dve.wait_ge(xt_ready, KB * (c - 1))
                for t in range(TB):
                    tile = c * TB + t
                    nc.vector.tensor_scalar(xn[:, c % 2, t, :], acc[:, tile, :], moments[:, tile, 0:1],
                                            rstd[:, tile:tile + 1], ALU.subtract,
                                            ALU.mult).then_inc(xn_done, 1)

            def xt_low(c):
                for kb in range(KB):
                    dve.wait_ge(xt_hi_done, c * KB + kb + 1)
                    nc.vector.tensor_tensor(xt_lo[:, kb, tokens(c)], bank[4 + kb][:],
                                            f32(xt_hi[:, kb, tokens(c)]),
                                            ALU.subtract).then_inc(xt_lo_done, 1)

            def hidden(r, n):
                dve.wait_ge(silu_done, in_pass(r, GU, n, GU))
                dve.wait_ge(up_ready, in_pass(r, GU, n))
                dve.wait_ge(h_lo_done, in_pass(r, GU, n - 2, GU))
                f = n // CHUNKS
                nc.vector.scalar_tensor_tensor(h32[:, n % 2, :], bank[2 + n % 2][:],
                                               us_sb[:, bass.ds(r * 2 + f, 1)], gated[:, n % 2, :],
                                               ALU.mult, ALU.mult).then_inc(h32_done, 1)

            def split_ff(r, tile):
                dve.wait_ge(fw_hi_done, in_pass(r, F_TILES, tile))
                nc.vector.tensor_tensor(fw_lo[:, tile, :], fraw[:, tile, :], f32(fw_hi[:, tile, :]),
                                        ALU.subtract).then_inc(fw_lo_done, 1)

            def ff_pass(r, has_next, with_rows=False):
                for n in range(GU):
                    if with_rows and n + 1 < CHUNKS:
                        if n + 2 < CHUNKS:
                            statistics(n + 2)
                        xt_low(n + 1)
                        if n + 2 < CHUNKS:
                            normalise(n + 2)
                    if with_rows and n == CHUNKS - 1:
                        for tile in (2, 3):
                            split_ff(0, tile)
                    hidden(r, n)
                    if n == CHUNKS:
                        for tile in (4, 5):
                            split_ff(r, tile)
                    if n == CHUNKS + 1 and has_next:
                        for tile in (0, 1):
                            split_ff(r + 1, tile)
                for m in range(TILES):
                    if m == 2 and has_next:
                        for tile in (2, 3):
                            split_ff(r + 1, tile)
                    dve.wait_ge(down_ready, in_pass(r, TILES, m))
                    dve.wait_ge(ff_added, in_pass(r, TILES, m - SCALED, TILES))
                    nc.vector.tensor_tensor(scaled[:, m % SCALED, :], bank[4 + m % 4][:], ds_sb[:],
                                            ALU.mult).then_inc(down_scaled, 1)

            statistics(0)
            normalise(0)
            for tile in (0, 1):
                split_ff(0, tile)
            xt_low(0)
            statistics(1)
            normalise(1)
            dve.wait_ge(scales_loaded, 48)
            ff_pass(0, True, with_rows=True)
            with dve.Fori(1, PAIRS - 1) as r:
                ff_pass(r, True)
            ff_pass(PAIRS - 1, False)

            def split_attention(g, tile):
                slot = tile % RAW
                dve.wait_ge(araw_loaded[slot], g * (16 * (W_TILES // RAW)) + (tile // RAW + 1) * 16)
                nc.vector.tensor_copy(aw_hi[:, tile, :], araw[:, slot, :]).then_inc(aw_hi_done, 1)

            def rotated(dst_g, c, j):
                return k_sb[:, c % 2, :] if j == K_TILE else q_sb[:, j - Q_TILE, :]

            def halves(ap):
                return ap.rearrange("p (b s) -> p b s", s=SEQ)

            def times_cos(g, c, j):
                dve.wait_ge(swapped, in_step(g, c, 1 + G, j))
                cos = rope_sb[:, 0:1, :].broadcast_to([P, CHUNK // SEQ, SEQ])
                nc.vector.tensor_tensor(halves(rotated(g, c, j)), halves(bank[j % 2][:]), cos,
                                        ALU.mult).then_inc(cos_done, 1)

            def add_sin(g, c, j):
                dve.wait_ge(sin_done, in_step(g, c, 1 + G, j))
                dve.wait_ge(cos_done, in_step(g, c, 1 + G, j))
                n = (1 + G) * c + j
                nc.vector.tensor_tensor(rotated(g, c, j), rotated(g, c, j), swap[:, n % 2, :],
                                        ALU.add).then_inc(qk_done, 1)

            def v_low(g, c):
                dve.wait_ge(v_hi_done, in_step(g, c, 1, 0))
                nc.vector.tensor_tensor(v_lo[:].rearrange("p t d -> p (t d)"), bank[AT_BANK][:],
                                        f32(v_hi[:]).rearrange("p t d -> p (t d)"),
                                        ALU.subtract).then_inc(v_done, 1)

            def masked_scores(g, c, b):
                for which in range(3):
                    ready = held(dve, in_step(g, c, 6, 3 * b + which))
                    dve.wait_ge(tables_loaded, 32)
                    dve.wait_ge(scores_ready, ready)
                    heads = (0, 1, 2, 3) if which == 2 else (2 * which, 2 * which + 1)
                    for h in heads:
                        if which == 2:
                            src, mask = bank[4][:, h * P:(h + 1) * P], mask_sb[:, 0:P]
                            dst, col = s_early[:, b, h, :], G + h
                        else:
                            src = bank[2 + which][:, (h % 2) * SEQ:(h % 2 + 1) * SEQ]
                            dst, col, mask = s_late[:, b, h, :], h, mask_sb[:, P:3 * P]
                        last = nc.vector.tensor_tensor_reduce(
                            out=dst, in0=src, in1=mask, scale=-SM_SCALE, scalar=BIGGEST, op0=ALU.add,
                            op1=ALU.min, accum_out=negmax[:, b, col:col + 1])
                    last.then_inc(scores_used, 1)

            def reciprocals(g, c, b):
                dve.wait_ge(exp_done, in_step(g, c, 6, 3 * b + 2))
                nc.vector.reciprocal(rsums[:, b, :], sums[:, b, :]).then_inc(rsums_done, 1)

            def pt_low(g, c, b, i):
                n = 3 * b + i
                dve.wait_ge(pt_hi_done, in_step(g, c, 6, n))
                nc.vector.tensor_tensor(pt_lo[:, i, :], bank[PT_BANK[n % 2]][:], f32(pt_hi[:, i, :]),
                                        ALU.subtract).then_inc(pt_done, 1)

            def at_low(g, c, b, late):
                dve.wait_ge(at_hi_done, in_step(g, c, 4, 2 * b + late))
                nc.vector.tensor_tensor(at_lo[:, late, :], bank[AT_BANK][:], f32(at_hi[:, late, :]),
                                        ALU.subtract).then_inc(at_done, 1)

            def add_output(g, c, n):
                dve.wait_ge(wo_ready, in_step(g, c, TB, n))
                tile = c * TB + n
                nc.vector.tensor_tensor(acc[:, tile, :], bank[n % 2][:], acc[:, tile, :],
                                        ALU.add).then_inc(wo_added, 1)

            def step(g, c, has_next):
                ng, nxt = (g, c + 1) if c + 1 < CHUNKS else (g + 1, 0)
                refill = c == CHUNKS - 2 and not (isinstance(g, int) and g == KV_HEADS - 1)

                def rotate_half(j):
                    times_cos(ng, nxt, j)
                    if refill:
                        split_attention(g + 1, j)

                masked_scores(g, c, 0)
                if c == 0:
                    for tile in range(O_TILE, W_TILES):
                        split_attention(g, tile)
                if has_next:
                    rotate_half(K_TILE)
                masked_scores(g, c, 1)
                reciprocals(g, c, 0)
                if has_next:
                    add_sin(ng, nxt, K_TILE)
                    rotate_half(Q_TILE)
                    rotate_half(Q_TILE + 1)
                reciprocals(g, c, 1)
                if has_next:
                    add_sin(ng, nxt, Q_TILE)
                    rotate_half(Q_TILE + 2)
                    add_sin(ng, nxt, Q_TILE + 1)
                pt_low(g, c, 0, 0)
                pt_low(g, c, 0, 1)
                if has_next:
                    rotate_half(Q_TILE + 3)
                    add_sin(ng, nxt, Q_TILE + 2)
                pt_low(g, c, 0, 2)
                at_low(g, c, 0, 0)
                if has_next:
                    add_sin(ng, nxt, Q_TILE + 3)
                pt_low(g, c, 1, 0)
                at_low(g, c, 0, 1)
                pt_low(g, c, 1, 1)
                pt_low(g, c, 1, 2)
                add_output(g, c, 0)
                at_low(g, c, 1, 0)
                add_output(g, c, 1)
                at_low(g, c, 1, 1)
                add_output(g, c, 2)
                if has_next:
                    v_low(ng, nxt)
                if refill:
                    split_attention(g + 1, V_TILE)
                add_output(g, c, 3)

            dve.wait_ge(tables_loaded, 32)
            for tile in range(IN_TILES):
                split_attention(0, tile)
                dve.wait_ge(aw_hi_done, tile + 1)
                nc.vector.tensor_tensor(aw_lo[:, tile, :], araw[:, tile % RAW, :], f32(aw_hi[:, tile, :]),
                                        ALU.subtract).then_inc(aw_lo_done, 1)
            times_cos(0, 0, 0)
            for j in range(1, 1 + G):
                times_cos(0, 0, j)
                add_sin(0, 0, j - 1)
            add_sin(0, 0, G)
            v_low(0, 0)
            with dve.Fori(0, KV_HEADS - 1) as g:
                for c in range(CHUNKS):
                    step(g, c, True)
            for c in range(CHUNKS):
                step(KV_HEADS - 1, c, c < CHUNKS - 1)

        @block.gpsimd
        def _(pool):
            nc.gpsimd.memset(power[:], -0.5).then_inc(power_set, 1)
            pool.wait_ge(power_set, 1)
            for c in range(CHUNKS):
                cols = slice(c * TB, (c + 1) * TB)
                pool.wait_ge(eps_added, c + 1)
                nc.gpsimd.tensor_tensor(rstd[:, cols], var_eps[:, cols], power[:],
                                        ALU.pow).then_inc(rstd_done, 1)

            def spread_peak(which, count):
                found = held(pool, count)
                pool.wait_ge(peak_done, 1)
                pool.wait_ge(peak_done, found)
                nc.gpsimd.partition_all_reduce(flags[:, which:which + 1], peaks[:, which:which + 1], P,
                                               bass.bass_isa.ReduceOp.max).then_inc(flag_done, 1)

            def ff_pass(r, has_next, first=False):
                for n in range(GU):
                    if first and n == 2:
                        spread_peak(GATE_UP, 1)
                    if n == CHUNKS + 2:
                        spread_peak(DOWN, in_pass(r, 2, 1))
                    pool.wait_ge(h_hi_done, in_pass(r, GU, n))
                    cols = (slice(None), n // CHUNKS, tokens(n % CHUNKS))
                    nc.gpsimd.tensor_tensor(h_lo[cols], h32[:, n % 2, :], f32(h_hi[cols]),
                                            ALU.subtract).then_inc(h_lo_done, 1)
                for m in range(TILES):
                    if m == 4 and has_next:
                        spread_peak(GATE_UP, in_pass(r + 1, 2, 0))
                    pool.wait_ge(down_scaled, in_pass(r, TILES, m, TILES))
                    pool.wait_ge(ff_added, in_pass(r, TILES, m - TILES, TILES))
                    nc.gpsimd.tensor_tensor(acc[:, m, :], acc[:, m, :], scaled[:, m % SCALED, :],
                                            ALU.add).then_inc(ff_added, 1)

            pool.wait_ge(xn_done, TILES)
            ff_pass(0, True, first=True)
            with pool.Fori(1, PAIRS - 1) as r:
                ff_pass(r, True)
            ff_pass(PAIRS - 1, False)

            def split_attention(g, tile):
                pool.wait_ge(aw_hi_done, g * W_TILES + (tile + 1))
                nc.gpsimd.tensor_tensor(aw_lo[:, tile, :], araw[:, tile % RAW, :], f32(aw_hi[:, tile, :]),
                                        ALU.subtract).then_inc(aw_lo_done, 1)

            def times_sin(g, c, j):
                n = (1 + G) * c + j
                pool.wait_ge(swapped, in_step(g, c, 1 + G, j))
                s = swap[:, n % 2, :].rearrange("p (b s) -> p b s", s=SEQ)
                sin = rope_sb[:, 1:2, :].broadcast_to([P, CHUNK // SEQ, SEQ])
                nc.gpsimd.tensor_tensor(s, s, sin, ALU.mult).then_inc(sin_done, 1)

            def normalise(g, c, b):
                pool.wait_ge(rsums_done, in_step(g, c, 2, b))
                for s, cols in ((s_early, slice(G, 2 * G)), (s_late, slice(0, G))):
                    keys = s.shape[-1]
                    r = rsums[:, b, cols].unsqueeze(2).broadcast_to([P, G, keys])
                    nc.gpsimd.tensor_tensor(s[:, b, :, :], s[:, b, :, :], r, ALU.mult).then_inc(probs_done, 1)

            def step(g, c, has_next):
                ng, nxt = (g, c + 1) if c + 1 < CHUNKS else (g + 1, 0)
                refill = c == CHUNKS - 2 and not (isinstance(g, int) and g == KV_HEADS - 1)
                if c == 0:
                    for tile in range(O_TILE, W_TILES):
                        split_attention(g, tile)
                if has_next:
                    times_sin(ng, nxt, K_TILE)
                normalise(g, c, 0)
                if refill:
                    split_attention(g + 1, K_TILE)
                if has_next:
                    times_sin(ng, nxt, Q_TILE)
                    times_sin(ng, nxt, Q_TILE + 1)
                normalise(g, c, 1)
                if refill:
                    split_attention(g + 1, Q_TILE)
                if has_next:
                    times_sin(ng, nxt, Q_TILE + 2)
                    times_sin(ng, nxt, Q_TILE + 3)
                if refill:
                    for tile in range(Q_TILE + 1, IN_TILES):
                        split_attention(g + 1, tile)

            pool.wait_ge(tables_loaded, 32)
            for j in range(1 + G):
                times_sin(0, 0, j)
            with pool.Fori(0, KV_HEADS - 1) as g:
                for c in range(CHUNKS):
                    step(g, c, True)
            for c in range(CHUNKS):
                step(KV_HEADS - 1, c, c < CHUNKS - 1)


def kernel(L0_attn_x, L0_attn_wq, L0_attn_wk, L0_attn_wv, L0_attn_wo, L0_ffn_gate_t, L0_ffn_up_t,
           L0_ffn_down_t, L0_ffn_gate_s, L0_ffn_up_s, L0_ffn_down_s):
    import concourse.bacc as bacc
    from concourse.bass_utils import run_bass_kernel_spmd

    def columns(w, blocks):
        w = np.asarray(w).reshape(KB, P, blocks, P)
        return np.ascontiguousarray(w.transpose(2, 1, 0, 3)).reshape(blocks, P, KB * P)

    def rows(w):
        return np.ascontiguousarray(w).reshape(-1, P, HID)

    data = {
        "x": np.asarray(L0_attn_x).reshape(TOKENS, HID),
        "wq": columns(L0_attn_wq, Q_HEADS),
        "wk": columns(L0_attn_wk, KV_HEADS),
        "wv": columns(L0_attn_wv, KV_HEADS),
        "wo": rows(np.asarray(L0_attn_wo)),
        "gate": columns(np.asarray(L0_ffn_gate_t).T, FBLOCKS),
        "up": columns(np.asarray(L0_ffn_up_t).T, FBLOCKS),
        "down": rows(np.asarray(L0_ffn_down_t).T),
        "gate_s": np.ascontiguousarray(np.asarray(L0_ffn_gate_s).reshape(FBLOCKS, P).T),
        "up_s": np.ascontiguousarray(np.asarray(L0_ffn_up_s).reshape(FBLOCKS, P).T),
        "down_s": np.asarray(L0_ffn_down_s),
        "rope": rope_tables(),
        "masks": score_masks(),
        "ident": np.eye(P, dtype=np.float32),
    }
    nc = bacc.Bacc("TRN2", target_bir_lowering=False, num_devices=1)
    aps = [nc.dram_tensor(n, a.shape, mybir.dt.from_np(a.dtype), kind="ExternalInput").ap()
           for n, a in data.items()]
    out = nc.dram_tensor("out", (TOKENS, HID), F32, kind="ExternalOutput").ap()
    block_kernel(nc, *aps, out)
    result = run_bass_kernel_spmd(nc, [data], core_ids=[0])
    return result.results[0]["out"].reshape(BATCH, SEQ, HID)
```

```python
from contextlib import ExitStack

import concourse.bass as bass
import numpy as np
from concourse import mybir

F32 = mybir.dt.float32
F32R = mybir.dt.float32r
I32 = mybir.dt.int32
BF16 = mybir.dt.bfloat16
ACT = mybir.ActivationFunctionType
ALU = mybir.AluOpType
AX = mybir.AxisListType

P = 128
BATCH, SEQ, HID = 8, 256, 512
TOKENS = BATCH * SEQ
FF = 1792
Q_HEADS, KV_HEADS, DH = 32, 8, 128
HALF = DH // 2
WINDOW = 128
THETA = 10000.0
EPS = 1e-5
SM_SCALE = DH ** -0.5
MASKED = -3.0e38
BIGGEST = 3.4e38

KB = HID // P
CHUNK = 512
CHUNKS = TOKENS // CHUNK
TB = CHUNK // P
G = Q_HEADS // KV_HEADS
FBLOCKS = FF // P
PAIRS = FBLOCKS // 2
TILES = TOKENS // P

K_TILE, Q_TILE, V_TILE, O_TILE = 0, 1, 1 + G, 2 + G
IN_TILES, W_TILES = 2 + G, 2 + 2 * G
RAW = 5
F_TILES = 6


def rope_tables():
    inv_freq = np.float32(THETA) ** (-np.arange(HALF, dtype=np.float32) / np.float32(HALF))
    angle = np.arange(SEQ, dtype=np.float32)[None, :] * inv_freq.astype(np.float32)[:, None]
    cos, sin = np.cos(angle), np.sin(angle)
    return np.concatenate([np.concatenate([cos, cos]), np.concatenate([-sin, sin])], axis=1).astype(np.float32)


def score_masks():
    i, j = np.arange(P)[:, None], np.arange(P)[None, :]
    causal = np.where(j <= i, 0.0, MASKED)
    window = np.where(j > i + P - WINDOW, 0.0, MASKED)
    return np.concatenate([causal, window, causal], axis=1).astype(np.float32)


def key_sides():
    j, i = np.arange(P)[:, None], np.arange(P)[None, :]
    return np.concatenate([j > i, j <= i], axis=1).astype(np.float32)


def block_kernel(nc, x, wq, wk, wv, wo, gate, up, down, gate_s, up_s, down_s, rope, masks, sides, ident, out):
    with ExitStack() as ctx:
        def sem(name):
            return ctx.enter_context(nc.semaphore(name))

        def tensors(stack, **shapes):
            return [stack.enter_context(nc.sbuf_tensor(n, s, d)) for n, (s, d) in shapes.items()]

        xt_hi, xt_lo, acc, rope_sb, mask_sb, side_sb, ident_sb = tensors(
            ctx, xt_hi=([P, KB, TOKENS], F32R), xt_lo=([P, KB, TOKENS], F32R),
            acc=([P, TILES, HID], F32), rope_sb=([P, 2, SEQ], F32), mask_sb=([P, 3 * P], F32),
            side_sb=([P, 2, P], F32), ident_sb=([P, P], F32))
        with ExitStack() as ff:
            (gu_hi, d_hi, d_lo, magnitudes, gu_lo, h_hi, h_lo, gs_sb, us_sb, ds_sb, fraw, stats, moments, var_eps,
             power, rstd, peaks, flags, xn, gated, h32) = tensors(
                ff, gu_hi=([P, 4, 512], F32R), d_hi=([P, 2, 512], F32R), d_lo=([P, 2, 512], F32R),
                magnitudes=([P, 4, 512], BF16), gu_lo=([P, 4, 512], F32R),
                h_hi=([P, 2, TOKENS], F32R), h_lo=([P, 2, TOKENS], F32R),
                gs_sb=([P, FBLOCKS], F32), us_sb=([P, FBLOCKS], F32), ds_sb=([P, HID], F32),
                fraw=([P, F_TILES, 512], I32),
                stats=([P, TILES, 6], F32),
                moments=([P, TILES, 2], F32), var_eps=([P, TILES], F32), power=([P, TB], F32),
                rstd=([P, TILES], F32), peaks=([P, 2], F32), flags=([P, 2], F32),
                xn=([P, 2, TB, HID], F32), gated=([P, 2, CHUNK], F32),
                h32=([P, 2, CHUNK], F32))
        (aw_hi, aw_lo, q_sb, k_sb, swap, vt_sb, v_hi, v_lo, s_late, s_early, pt_hi, pt_lo, at_hi, at_lo,
         negmax, sums, rsums, araw) = tensors(
            ctx, aw_hi=([P, W_TILES, 512], F32R), aw_lo=([P, W_TILES, 512], F32R),
            q_sb=([P, G, CHUNK], F32), k_sb=([P, 2, CHUNK], F32), swap=([P, 2, CHUNK], F32),
            vt_sb=([P, CHUNK], F32), v_hi=([P, TB, DH], F32R), v_lo=([P, TB, DH], F32R),
            s_late=([P, 2, G, 2 * P], F32), s_early=([P, 2, G, P], F32),
            pt_hi=([P, 3, G * P], F32R), pt_lo=([P, 3, G * P], F32R),
            at_hi=([P, 2, G * P], F32R), at_lo=([P, 2, G * P], F32R),
            negmax=([P, 2, 2 * G], F32), sums=([P, 2, 2 * G], F32), rsums=([P, 2, 2 * G], F32),
            araw=([P, RAW, 512], F32))
        scaled = xn[:].rearrange("p a t h -> p (a t) h")
        SCALED = 2 * TB
        bank = [ctx.enter_context(nc.psum_tensor(f"bank{i}", [P, 512], F32)) for i in range(8)]

        x_loaded = [[sem(f"x_loaded{c}_{t}") for t in range(TB)] for c in range(CHUNKS)]
        ident_loaded, scales_loaded, tables_loaded = sem("ident_loaded"), sem("scales_loaded"), sem("tables_loaded")
        stats_done, moments_done, eps_added = sem("stats_done"), sem("moments_done"), sem("eps_added")
        power_set, rstd_done, xn_done = sem("power_set"), sem("rstd_done"), sem("xn_done")
        xt_ready, xt_hi_done, xt_lo_done = sem("xt_ready"), sem("xt_hi_done"), sem("xt_lo_done")
        fraw_loaded = [sem(f"fraw_loaded{i}") for i in range(F_TILES)]
        fw_hi_done, fw_lo_done = sem("fw_hi_done"), sem("fw_lo_done")
        peak_done, flag_done = sem("peak_done"), sem("flag_done")
        gate_ready, up_ready, silu_done, h32_done = sem("gate_ready"), sem("up_ready"), sem("silu_done"), sem("h32_done")
        h_hi_done, h_lo_done = sem("h_hi_done"), sem("h_lo_done")
        down_ready, down_scaled, ff_added = sem("down_ready"), sem("down_scaled"), sem("ff_added")
        araw_loaded = [sem(f"araw_loaded{i}") for i in range(RAW)]
        aw_hi_done, aw_lo_done = sem("aw_hi_done"), sem("aw_lo_done")
        proj_ready, swapped, cos_done, sin_done, qk_done = (
            sem("proj_ready"), sem("swapped"), sem("cos_done"), sem("sin_done"), sem("qk_done"))
        vt_done, v_ready, v_hi_done, v_done = sem("vt_done"), sem("v_ready"), sem("v_hi_done"), sem("v_done")
        scores_ready, scores_used, exp_done = sem("scores_ready"), sem("scores_used"), sem("exp_done")
        rsums_done, probs_done = sem("rsums_done"), sem("probs_done")
        late_merged, pt_ready, pt_hi_done, pt_done = (
            sem("late_merged"), sem("pt_ready"), sem("pt_hi_done"), sem("pt_done"))
        hi_parted, lo_parted = sem("hi_parted"), sem("lo_parted")
        at_ready, at_hi_done, at_done = sem("at_ready"), sem("at_hi_done"), sem("at_done")
        wo_ready, wo_added, stored = sem("wo_ready"), sem("wo_added"), sem("stored")

        def in_pass(r, per_pass, item, before=0):
            return r * per_pass + (item + 1 + before)

        def in_step(g, c, per_step, item, before=0):
            return g * (CHUNKS * per_step) + (c * per_step + item + 1 + before)

        def puts_off(g, c):
            return isinstance(g, int) and (g, c) == (KV_HEADS - 1, CHUNKS - 2)

        def held(engine, count):
            return count if isinstance(count, int) else engine.to_reg(count)

        def tokens(c):
            return slice(c * CHUNK, (c + 1) * CHUNK)

        def f32(ap):
            return ap.bitcast(F32)

        def parted(pt):
            return [pt[:, i, :].rearrange("p (h i) -> p h i", h=G) for i in (1, 2)]

        def side(late):
            return side_sb[:, late:late + 1, :].broadcast_to([P, G, P])

        def weight_block(w, tile, kb):
            return w[:, tile, kb * P:(kb + 1) * P]

        def fw_hi(tile):
            return gu_hi[:, tile, :] if tile < 4 else d_hi[:, tile - 4, :]

        def fw_lo(tile):
            return gu_lo[:, tile, :] if tile < 4 else d_lo[:, tile - 4, :]

        GU = 2 * CHUNKS
        GATE_UP, DOWN = 0, 1
        PT_BANK = (5, 6)
        AT_BANK = 7

        block = ctx.enter_context(nc.Block())

        @block.sync
        def _(sp):
            x_v = x.rearrange("(c t p) h -> c p t h", c=CHUNKS, p=P)
            out_v = out.rearrange("(c t p) h -> c p t h", c=CHUNKS, p=P)
            def load_x(c):
                for t in range(TB):
                    sp.dma_start(acc[:, c * TB + t, :], x_v[c][:, t, :]).then_inc(x_loaded[c][t], 16)

            def load_ff(r, tile):
                src = (gate, up, gate, up, down, down)[tile]
                f = r * 2 + (0, 0, 1, 1, 0, 1)[tile]
                sp.dma_start(fraw[:, tile, :], src[f]).then_inc(fraw_loaded[tile], 16)

            load_x(0)
            sp.dma_start(ident_sb[:], ident).then_inc(ident_loaded, 16)
            for tile in (0, 1):
                load_ff(0, tile)
            load_x(1)
            for dst, src in ((gs_sb, gate_s), (us_sb, up_s)):
                sp.dma_start(dst[:], src).then_inc(scales_loaded, 16)
            sp.dma_start(ds_sb[:], down_s.partition_broadcast(P)).then_inc(scales_loaded, 16)
            load_x(2)
            for tile in (2, 3):
                load_ff(0, tile)
            load_x(3)
            for tile in (4, 5):
                load_ff(0, tile)
            sp.dma_start(rope_sb[:].rearrange("p a s -> p (a s)"), rope).then_inc(tables_loaded, 16)
            sp.dma_start(mask_sb[:], masks).then_inc(tables_loaded, 16)
            sp.dma_start(side_sb[:].rearrange("p a i -> p (a i)"), sides).then_inc(tables_loaded, 16)
            with sp.Fori(0, PAIRS - 1) as r:
                for tile in range(F_TILES):
                    sp.wait_ge(fw_lo_done, in_pass(r, F_TILES, tile))
                    load_ff(r + 1, tile)

            def load_attention(g, tile):
                slot = tile % RAW
                if tile == K_TILE:
                    src = wk[g]
                elif tile < V_TILE:
                    src = wq[g * G + (tile - Q_TILE)]
                elif tile == V_TILE:
                    src = wv[g]
                else:
                    src = wo[g * G + (tile - O_TILE)]
                sp.dma_start(araw[:, slot, :], src).then_inc(araw_loaded[slot], 16)

            sp.wait_ge(h_lo_done, GU * (PAIRS + 1))
            for tile in range(RAW):
                load_attention(0, tile)
            for tile in range(RAW, W_TILES):
                sp.wait_ge(aw_lo_done, tile - RAW + 1)
                load_attention(0, tile)
            with sp.Fori(0, KV_HEADS - 1) as g:
                for tile in range(W_TILES):
                    sp.wait_ge(aw_lo_done, g * W_TILES + (W_TILES + tile - RAW + 1))
                    load_attention(g + 1, tile)

            for c in range(CHUNKS):
                for t in range(TB):
                    sp.wait_ge(wo_added, in_step(KV_HEADS - 1, c, TB, t, TB))
                    sp.dma_start(out_v[c][:, t, :], acc[:, c * TB + t, :]).then_inc(stored, 16)
            sp.wait_ge(stored, 16 * TILES)

        @block.tensor
        def _(pe):
            def product(dst, w_hi, w_lo, x_hi, x_lo, first, last, w_lo_too=True, x_lo_too=True):
                passes = [(w_hi, x_hi)] + [(w_hi, x_lo)] * x_lo_too + [(w_lo, x_hi)] * w_lo_too
                for n, (w, v) in enumerate(passes):
                    mm = nc.tensor.matmul(dst, w, v, start=first and n == 0,
                                          stop=last and n == len(passes) - 1)
                return mm

            def transpose_rows(c):
                pe.wait_ge(xn_done, TB * (c + 1))
                for kb in range(KB):
                    n = c * KB + kb
                    if c > 0:
                        pe.wait_ge(xt_lo_done, n - KB + 1)
                    for t in range(TB):
                        last = nc.tensor.transpose(bank[4 + kb][:, t * P:(t + 1) * P],
                                                   xn[:, c % 2, t, kb * P:(kb + 1) * P], ident_sb[:])
                    last.then_inc(xt_ready, 1)

            def gate_or_up(r, f, c, which, with_lo):
                n = f * CHUNKS + c
                ready, free = ((gate_ready, silu_done), (up_ready, h32_done))[which]
                if c == 0:
                    pe.wait_ge(fw_lo_done, in_pass(r, F_TILES, 2 * f + which))
                pe.wait_ge(free, in_pass(r, GU, n - 2, GU))
                for kb in range(KB):
                    last = product(bank[2 * which + n % 2][:], weight_block(gu_hi, 2 * f + which, kb),
                                   weight_block(gu_lo, 2 * f + which, kb), xt_hi[:, kb, tokens(c)],
                                   xt_lo[:, kb, tokens(c)], kb == 0, kb == KB - 1, w_lo_too=with_lo)
                last.then_inc(ready, 1)

            def gates_and_ups(r, blocks, with_lo):
                for f in blocks:
                    for c in range(CHUNKS):
                        for which in range(2):
                            gate_or_up(r, f, c, which, with_lo)

            def downs(r, with_lo):
                for m in range(TILES):
                    c = m // TB
                    if m % TB == 0:
                        pe.wait_ge(h_lo_done, in_pass(r, GU, CHUNKS + c, GU))
                    pe.wait_ge(down_scaled, in_pass(r, TILES, m - 4, TILES))
                    rows = slice(m * P, (m + 1) * P)
                    for f in range(2):
                        last = product(bank[4 + m % 4][:], h_hi[:, f, rows], h_lo[:, f, rows],
                                       d_hi[:, f, :], d_lo[:, f, :], f == 0, f == 1,
                                       x_lo_too=with_lo)
                    last.then_inc(down_ready, 1)

            def by_flag(r, which, work):
                known = held(pe, in_pass(r, 2, 0 if which == GATE_UP else 1))
                pe.wait_ge(flag_done, 1)
                pe.wait_ge(flag_done, known)
                biggest_lo = pe.value_load(flags[0:1, which:which + 1].bitcast(I32))
                with pe.If_ne(pe.to_reg(biggest_lo), 0):
                    work(True)
                with pe.Else():
                    work(False)

            def ff_pass(r, blocks):
                by_flag(r, GATE_UP, lambda with_lo: gates_and_ups(r, blocks, with_lo))
                by_flag(r, DOWN, lambda with_lo: downs(r, with_lo))

            pe.wait_ge(ident_loaded, 16)
            transpose_rows(0)
            for c in range(CHUNKS):
                pe.wait_ge(xt_lo_done, KB * (c + 1))
                gate_or_up(0, 0, c, 0, True)
                if c + 1 < CHUNKS:
                    transpose_rows(c + 1)
                gate_or_up(0, 0, c, 1, True)
            ff_pass(0, (1,))
            with pe.Fori(1, PAIRS) as r:
                ff_pass(r, (0, 1))

            def project(g, c, j):
                if c == 0:
                    pe.wait_ge(aw_lo_done, g * W_TILES + (j + 1))
                if j >= 2:
                    pe.wait_ge(cos_done, in_step(g, c, 1 + G, j - 2))
                for kb in range(KB):
                    last = product(bank[j % 2][:], weight_block(aw_hi, j, kb), weight_block(aw_lo, j, kb),
                                   xt_hi[:, kb, tokens(c)], xt_lo[:, kb, tokens(c)], kb == 0, kb == KB - 1)
                last.then_inc(proj_ready, 1)

            def project_next(g, c, j):
                if j < 2:
                    pe.wait_ge(wo_added, in_step(g, c - 1, TB, 2 + j, TB))
                if c + 1 < CHUNKS:
                    project(g, c + 1, j)
                else:
                    project(g + 1, 0, j)

            def transpose_v():
                for t in range(TB):
                    last = nc.tensor.transpose(bank[AT_BANK][:, t * DH:(t + 1) * DH],
                                               vt_sb[:, t * P:(t + 1) * P], ident_sb[:])
                last.then_inc(v_ready, 1)

            def scores(g, c, b):
                if b == 0:
                    pe.wait_ge(qk_done, in_step(g, c, 1 + G, G))
                early, late = b * SEQ, b * SEQ + P
                keys = k_sb[:, c % 2, b * SEQ:(b + 1) * SEQ]
                for pair in range(G // 2):
                    pe.wait_ge(scores_used, in_step(g, c, 6, 3 * b + pair - 3, 6))
                    for h in (2 * pair, 2 * pair + 1):
                        last = nc.tensor.matmul(bank[2 + pair][:, (h % 2) * SEQ:(h % 2 + 1) * SEQ],
                                                q_sb[:, h, late:late + P], keys, start=True, stop=True)
                    last.then_inc(scores_ready, 1)
                pe.wait_ge(scores_used, in_step(g, c, 6, 3 * b - 1, 6))
                for h in range(G):
                    last = nc.tensor.matmul(bank[4][:, h * P:(h + 1) * P], q_sb[:, h, early:early + P],
                                            keys[:, 0:P], start=True, stop=True)
                last.then_inc(scores_ready, 1)

            def transpose_probs(g, c, b, late):
                n = 2 * b + late
                pe.wait_ge(probs_done, in_step(g, c, 4, n))
                pe.wait_ge(pt_done, in_step(g, c, 4, n - 2, 4))
                for h in range(G):
                    src = s_late[:, b, h, 0:P] if late else s_early[:, b, h, :]
                    last = nc.tensor.transpose(bank[PT_BANK[late]][:, h * P:(h + 1) * P], src, ident_sb[:])
                last.then_inc(pt_ready, 1)

            def attend(g, c, b, late):
                n = 2 * b + late
                if late:
                    pe.wait_ge(hi_parted, in_step(g, c, 2, b))
                    pe.wait_ge(lo_parted, in_step(g, c, 2, b))
                else:
                    pe.wait_ge(pt_done, in_step(g, c, 4, n, 4))
                if n == 0:
                    pe.wait_ge(v_done, in_step(g, c, 1, 0))
                else:
                    pe.wait_ge(at_done, in_step(g, c, 4, n - 1))
                tiles = ((1, 2 * b), (2, 2 * b + 1)) if late else ((0, 2 * b),)
                for k, (i, t) in enumerate(tiles):
                    last = product(bank[AT_BANK][:], v_hi[:, t, :], v_lo[:, t, :], pt_hi[:, i, :],
                                   pt_lo[:, i, :], k == 0, k == len(tiles) - 1)
                last.then_inc(at_ready, 1)

            def output(g, c, b, late, has_next):
                n = 2 * b + late
                pe.wait_ge(at_done, in_step(g, c, 4, n))
                if n == 0 and c == 0:
                    pe.wait_ge(aw_lo_done, g * W_TILES + W_TILES)
                if n >= 2:
                    pe.wait_ge(wo_added, in_step(g, c, TB, n - 2, TB))
                elif not has_next:
                    pe.wait_ge(wo_added, in_step(g, c - 1, TB, n + 2, TB))
                elif n == 0:
                    pe.wait_ge(cos_done, in_step(g, c + 1, 1 + G, G))
                else:
                    pe.wait_ge(vt_done, in_step(g, c + 1, 1, 0))
                for h in range(G):
                    last = product(bank[n % 2][:], at_hi[:, late, h * P:(h + 1) * P],
                                   at_lo[:, late, h * P:(h + 1) * P], aw_hi[:, O_TILE + h, :],
                                   aw_lo[:, O_TILE + h, :], h == 0, h == G - 1)
                last.then_inc(wo_ready, 1)

            def step(g, c, has_next):
                ng, nxt = (g, c + 1) if c + 1 < CHUNKS else (g + 1, 0)
                if has_next:
                    project_next(g, c, K_TILE)
                scores(g, c, 1)
                if has_next:
                    for h in range(G - 1):
                        project_next(g, c, Q_TILE + h)
                else:
                    output(g, c - 1, 1, 0, True)
                transpose_probs(g, c, 0, 0)
                transpose_probs(g, c, 0, 1)
                if not has_next:
                    output(g, c - 1, 1, 1, True)
                if has_next:
                    project_next(g, c, Q_TILE + G - 1)
                attend(g, c, 0, 0)
                if has_next:
                    project_next(g, c, V_TILE)
                transpose_probs(g, c, 1, 0)
                attend(g, c, 0, 1)
                transpose_probs(g, c, 1, 1)
                output(g, c, 0, 0, has_next)
                attend(g, c, 1, 0)
                output(g, c, 0, 1, has_next)
                if not puts_off(g, c):
                    output(g, c, 1, 0, has_next)
                attend(g, c, 1, 1)
                if has_next:
                    scores(ng, nxt, 0)
                    pe.wait_ge(vt_done, in_step(g, c + 1, 1, 0))
                    pe.wait_ge(at_done, in_step(g, c, 4, 3))
                    transpose_v()
                if not puts_off(g, c):
                    output(g, c, 1, 1, has_next)

            for j in range(IN_TILES):
                project(0, 0, j)
            pe.wait_ge(vt_done, 1)
            pe.wait_ge(down_scaled, TILES * (PAIRS + 1))
            scores(0, 0, 0)
            transpose_v()
            with pe.Fori(0, KV_HEADS - 1) as g:
                for c in range(CHUNKS):
                    step(g, c, True)
            for c in range(CHUNKS):
                step(KV_HEADS - 1, c, c < CHUNKS - 1)

        @block.scalar
        def _(act):
            def xt_high(c):
                for kb in range(KB):
                    act.wait_ge(xt_ready, c * KB + kb + 1)
                    nc.scalar.activation(xt_hi[:, kb, tokens(c)], bank[4 + kb][:],
                                         ACT.Copy).then_inc(xt_hi_done, 1)

            def split_ff(r, tile):
                act.wait_ge(fraw_loaded[tile], r * 16 + 16)
                nc.scalar.activation(fw_hi(tile), fraw[:, tile, :], ACT.Copy).then_inc(fw_hi_done, 1)

            def h_high(r, n):
                act.wait_ge(h32_done, in_pass(r, GU, n, GU))
                nc.scalar.activation(h_hi[:, n // CHUNKS, tokens(n % CHUNKS)], h32[:, n % 2, :],
                                     ACT.Copy).then_inc(h_hi_done, 1)

            def find_peak(r, which):
                lo, last = (gu_lo, 3) if which == GATE_UP else (d_lo, 5)
                act.wait_ge(fw_lo_done, in_pass(r, F_TILES, last))
                nc.scalar.activation(magnitudes[:, 0:lo.shape[1], :], f32(lo[:]),
                                     ACT.Abs, accum_out=peaks[:, which:which + 1]).then_inc(peak_done, 1)

            def ff_pass(r, has_next, with_rows=False):
                for n in range(GU):
                    if with_rows and n + 1 < CHUNKS:
                        xt_high(n + 1)
                    slot_read = held(act, in_pass(r, GU, n - 2, GU))
                    ready = held(act, in_pass(r, GU, n))
                    act.wait_ge(scales_loaded, 48)
                    act.wait_ge(gate_ready, ready)
                    act.wait_ge(h32_done, slot_read)
                    f = n // CHUNKS
                    nc.scalar.activation(gated[:, n % 2, :], bank[n % 2][:], ACT.Silu,
                                         scale=gs_sb[:, bass.ds(r * 2 + f, 1)]).then_inc(silu_done, 1)
                    if n > 0:
                        h_high(r, n - 1)
                    if with_rows and n == CHUNKS - 2:
                        find_peak(0, GATE_UP)
                    if n == CHUNKS + 1:
                        find_peak(r, DOWN)
                    if with_rows and n == 0:
                        for tile in (2, 3):
                            split_ff(0, tile)
                    if n == (1 if with_rows else 0):
                        for tile in (4, 5):
                            split_ff(r, tile)
                    if n == CHUNKS and has_next:
                        act.wait_ge(up_ready, in_pass(r, GU, n - 1))
                        for tile in (0, 1):
                            split_ff(r + 1, tile)
                h_high(r, GU - 1)
                if has_next:
                    act.wait_ge(up_ready, in_pass(r, GU, GU - 1))
                    for tile in (2, 3):
                        split_ff(r + 1, tile)
                    find_peak(r + 1, GATE_UP)

            for tile in (0, 1):
                split_ff(0, tile)
            xt_high(0)
            ff_pass(0, True, with_rows=True)
            with act.Fori(1, PAIRS - 1) as r:
                ff_pass(r, True)
            ff_pass(PAIRS - 1, False)

            def swap_halves(g, c, j):
                n = (1 + G) * c + j
                act.wait_ge(proj_ready, in_step(g, c, IN_TILES, j))
                if not (isinstance(g, int) and g == 0 and n < 2):
                    act.wait_ge(qk_done, in_step(g, c, 1 + G, j - 2))
                nc.scalar.activation(swap[0:HALF, n % 2, :], bank[j % 2][HALF:P, :], ACT.Copy)
                nc.scalar.activation(swap[HALF:P, n % 2, :], bank[j % 2][0:HALF, :],
                                     ACT.Copy).then_inc(swapped, 1)

            def copy_vt(g, c):
                act.wait_ge(proj_ready, in_step(g, c, IN_TILES, V_TILE))
                nc.scalar.activation(vt_sb[:], bank[V_TILE % 2][:], ACT.Copy).then_inc(vt_done, 1)

            def v_high(g, c):
                act.wait_ge(v_ready, in_step(g, c, 1, 0))
                nc.scalar.activation(v_hi[:].rearrange("p t d -> p (t d)"), bank[AT_BANK][:],
                                     ACT.Copy).then_inc(v_hi_done, 1)

            def exponentials(g, c, b, which):
                act.wait_ge(scores_used, in_step(g, c, 6, 3 * b + which, 6))
                heads = (0, 1, 2, 3) if which == 2 else (2 * which, 2 * which + 1)
                for h in heads:
                    s = s_early[:, b, h, :] if which == 2 else s_late[:, b, h, :]
                    col = h + (G if which == 2 else 0)
                    last = nc.scalar.activation(s, s, ACT.Exp, scale=-1.0, bias=negmax[:, b, col:col + 1],
                                                accum_out=sums[:, b, col:col + 1])
                last.then_inc(exp_done, 1)

            def pt_high(g, c, b, late):
                n = 2 * b + late
                act.wait_ge(pt_ready, in_step(g, c, 4, n))
                if b == 1:
                    act.wait_ge(at_ready, in_step(g, c, 4, late))
                nc.scalar.activation(pt_hi[:, late, :], bank[PT_BANK[late]][:],
                                     ACT.Copy).then_inc(pt_hi_done, 1)

            def at_high(g, c, b, late):
                n = 2 * b + late
                act.wait_ge(at_ready, in_step(g, c, 4, n))
                if b == 1:
                    act.wait_ge(wo_ready, in_step(g, c, TB, late))
                nc.scalar.activation(at_hi[:, late, :], bank[AT_BANK][:], ACT.Copy).then_inc(at_hi_done, 1)

            def step(g, c, has_next):
                ng, nxt = (g, c + 1) if c + 1 < CHUNKS else (g + 1, 0)
                for which in range(3):
                    exponentials(g, c, 0, which)
                if has_next:
                    swap_halves(ng, nxt, K_TILE)
                exponentials(g, c, 1, 0)
                exponentials(g, c, 1, 1)
                if has_next:
                    swap_halves(ng, nxt, Q_TILE)
                exponentials(g, c, 1, 2)
                if has_next:
                    swap_halves(ng, nxt, Q_TILE + 1)
                    swap_halves(ng, nxt, Q_TILE + 2)
                pt_high(g, c, 0, 0)
                pt_high(g, c, 0, 1)
                if has_next:
                    swap_halves(ng, nxt, Q_TILE + 3)
                at_high(g, c, 0, 0)
                if has_next:
                    copy_vt(ng, nxt)
                pt_high(g, c, 1, 0)
                at_high(g, c, 0, 1)
                pt_high(g, c, 1, 1)
                at_high(g, c, 1, 0)
                at_high(g, c, 1, 1)
                if has_next:
                    v_high(ng, nxt)

            for j in range(1 + G):
                swap_halves(0, 0, j)
            copy_vt(0, 0)
            v_high(0, 0)
            with act.Fori(0, KV_HEADS - 1) as g:
                for c in range(CHUNKS):
                    step(g, c, True)
            for c in range(CHUNKS):
                step(KV_HEADS - 1, c, c < CHUNKS - 1)

        @block.vector
        def _(dve):
            for s, n in ((silu_done, GU), (h32_done, GU), (h_lo_done, GU), (down_scaled, TILES),
                         (ff_added, TILES), (scores_used, 6), (pt_done, 4), (wo_added, TB)):
                dve.sem_inc(s, n)

            def statistics(c):
                for t in range(TB):
                    dve.wait_ge(x_loaded[c][t], 16)
                    last = nc.vector.bn_stats(stats[:, c * TB + t, :], acc[:, c * TB + t, :])
                last.then_inc(stats_done, 1)
                dve.wait_ge(stats_done, c + 1)
                for t in range(c * TB, (c + 1) * TB):
                    last = nc.vector.bn_aggr(moments[:, t, :], stats[:, t, :])
                last.then_inc(moments_done, 1)
                dve.wait_ge(moments_done, c + 1)
                cols = slice(c * TB, (c + 1) * TB)
                nc.vector.tensor_scalar(var_eps[:, cols], moments[:, cols, 1], EPS, None,
                                        ALU.add).then_inc(eps_added, 1)

            def normalise(c):
                dve.wait_ge(rstd_done, c + 1)
                if c >= 2:
                    dve.wait_ge(xt_ready, KB * (c - 1))
                for t in range(TB):
                    tile = c * TB + t
                    nc.vector.tensor_scalar(xn[:, c % 2, t, :], acc[:, tile, :], moments[:, tile, 0:1],
                                            rstd[:, tile:tile + 1], ALU.subtract,
                                            ALU.mult).then_inc(xn_done, 1)

            def xt_low(c):
                for kb in range(KB):
                    dve.wait_ge(xt_hi_done, c * KB + kb + 1)
                    nc.vector.tensor_tensor(xt_lo[:, kb, tokens(c)], bank[4 + kb][:],
                                            f32(xt_hi[:, kb, tokens(c)]),
                                            ALU.subtract).then_inc(xt_lo_done, 1)

            def hidden(r, n):
                dve.wait_ge(silu_done, in_pass(r, GU, n, GU))
                dve.wait_ge(up_ready, in_pass(r, GU, n))
                dve.wait_ge(h_lo_done, in_pass(r, GU, n - 2, GU))
                f = n // CHUNKS
                nc.vector.scalar_tensor_tensor(h32[:, n % 2, :], bank[2 + n % 2][:],
                                               us_sb[:, bass.ds(r * 2 + f, 1)], gated[:, n % 2, :],
                                               ALU.mult, ALU.mult).then_inc(h32_done, 1)

            def split_ff(r, tile):
                dve.wait_ge(fw_hi_done, in_pass(r, F_TILES, tile))
                nc.vector.tensor_tensor(fw_lo(tile), fraw[:, tile, :], f32(fw_hi(tile)),
                                        ALU.subtract).then_inc(fw_lo_done, 1)

            def split_attention(g, tile):
                slot = tile % RAW
                dve.wait_ge(araw_loaded[slot], g * (16 * (W_TILES // RAW)) + (tile // RAW + 1) * 16)
                nc.vector.tensor_copy(aw_hi[:, tile, :], araw[:, slot, :]).then_inc(aw_hi_done, 1)

            def split_first(tile):
                split_attention(0, tile)
                dve.wait_ge(aw_hi_done, tile + 1)
                nc.vector.tensor_tensor(aw_lo[:, tile, :], araw[:, tile % RAW, :], f32(aw_hi[:, tile, :]),
                                        ALU.subtract).then_inc(aw_lo_done, 1)

            def ff_pass(r, has_next, with_rows=False):
                for n in range(GU):
                    if with_rows and n + 1 < CHUNKS:
                        xt_low(n + 1)
                        if n + 2 < CHUNKS:
                            normalise(n + 2)
                        if n + 3 < CHUNKS:
                            statistics(n + 3)
                    hidden(r, n)
                    if with_rows and n == 1:
                        for tile in (2, 3):
                            split_ff(0, tile)
                    if n == CHUNKS:
                        for tile in (4, 5):
                            split_ff(r, tile)
                    if n == CHUNKS + 1 and has_next:
                        for tile in (0, 1):
                            split_ff(r + 1, tile)
                for m in range(TILES):
                    if m == 2 and has_next:
                        for tile in (2, 3):
                            split_ff(r + 1, tile)
                    if m >= 8 and m % 2 == 0 and not has_next:
                        split_first(m // 2 - 4)
                    dve.wait_ge(down_ready, in_pass(r, TILES, m))
                    dve.wait_ge(ff_added, in_pass(r, TILES, m - SCALED, TILES))
                    nc.vector.tensor_tensor(scaled[:, m % SCALED, :], bank[4 + m % 4][:], ds_sb[:],
                                            ALU.mult).then_inc(down_scaled, 1)

            statistics(0)
            split_ff(0, 0)
            normalise(0)
            statistics(1)
            xt_low(0)
            split_ff(0, 1)
            normalise(1)
            statistics(2)
            dve.wait_ge(scales_loaded, 48)
            ff_pass(0, True, with_rows=True)
            with dve.Fori(1, PAIRS - 1) as r:
                ff_pass(r, True)
            ff_pass(PAIRS - 1, False)

            def rotated(dst_g, c, j):
                return k_sb[:, c % 2, :] if j == K_TILE else q_sb[:, j - Q_TILE, :]

            def halves(ap):
                return ap.rearrange("p (b s) -> p b s", s=SEQ)

            def times_cos(g, c, j):
                dve.wait_ge(swapped, in_step(g, c, 1 + G, j))
                cos = rope_sb[:, 0:1, :].broadcast_to([P, CHUNK // SEQ, SEQ])
                nc.vector.tensor_tensor(halves(rotated(g, c, j)), halves(bank[j % 2][:]), cos,
                                        ALU.mult).then_inc(cos_done, 1)

            def add_sin(g, c, j):
                dve.wait_ge(sin_done, in_step(g, c, 1 + G, j))
                dve.wait_ge(cos_done, in_step(g, c, 1 + G, j))
                n = (1 + G) * c + j
                nc.vector.tensor_tensor(rotated(g, c, j), rotated(g, c, j), swap[:, n % 2, :],
                                        ALU.add).then_inc(qk_done, 1)

            def v_low(g, c):
                dve.wait_ge(v_hi_done, in_step(g, c, 1, 0))
                nc.vector.tensor_tensor(v_lo[:].rearrange("p t d -> p (t d)"), bank[AT_BANK][:],
                                        f32(v_hi[:]).rearrange("p t d -> p (t d)"),
                                        ALU.subtract).then_inc(v_done, 1)

            def masked_scores(g, c, b):
                for which in range(3):
                    ready = held(dve, in_step(g, c, 6, 3 * b + which))
                    dve.wait_ge(tables_loaded, 48)
                    dve.wait_ge(scores_ready, ready)
                    heads = (0, 1, 2, 3) if which == 2 else (2 * which, 2 * which + 1)
                    for h in heads:
                        if which == 2:
                            src, mask = bank[4][:, h * P:(h + 1) * P], mask_sb[:, 0:P]
                            dst, col = s_early[:, b, h, :], G + h
                        else:
                            src = bank[2 + which][:, (h % 2) * SEQ:(h % 2 + 1) * SEQ]
                            dst, col, mask = s_late[:, b, h, :], h, mask_sb[:, P:3 * P]
                        last = nc.vector.tensor_tensor_reduce(
                            out=dst, in0=src, in1=mask, scale=-SM_SCALE, scalar=BIGGEST, op0=ALU.add,
                            op1=ALU.min, accum_out=negmax[:, b, col:col + 1])
                    last.then_inc(scores_used, 1)

            def reciprocals(g, c, b):
                dve.wait_ge(exp_done, in_step(g, c, 6, 3 * b + 2))
                nc.vector.reciprocal(rsums[:, b, :], sums[:, b, :]).then_inc(rsums_done, 1)

            def pt_low(g, c, b, late):
                n = 2 * b + late
                dve.wait_ge(pt_hi_done, in_step(g, c, 4, n))
                nc.vector.tensor_tensor(pt_lo[:, late, :], bank[PT_BANK[late]][:], f32(pt_hi[:, late, :]),
                                        ALU.subtract).then_inc(pt_done, 1)

            def part_low(g, c, b):
                dve.wait_ge(pt_done, in_step(g, c, 4, 2 * b + 1, 4))
                early_keys, late_keys = parted(pt_lo)
                nc.vector.tensor_tensor(late_keys, f32(early_keys), side(1), ALU.mult)
                nc.vector.tensor_tensor(early_keys, f32(early_keys), side(0), ALU.mult).then_inc(lo_parted, 1)

            def at_low(g, c, b, late):
                dve.wait_ge(at_hi_done, in_step(g, c, 4, 2 * b + late))
                nc.vector.tensor_tensor(at_lo[:, late, :], bank[AT_BANK][:], f32(at_hi[:, late, :]),
                                        ALU.subtract).then_inc(at_done, 1)

            def add_output(g, c, n):
                dve.wait_ge(wo_ready, in_step(g, c, TB, n))
                tile = c * TB + n
                nc.vector.tensor_tensor(acc[:, tile, :], bank[n % 2][:], acc[:, tile, :],
                                        ALU.add).then_inc(wo_added, 1)

            def step(g, c, has_next):
                ng, nxt = (g, c + 1) if c + 1 < CHUNKS else (g + 1, 0)
                refill = c == CHUNKS - 2 and not (isinstance(g, int) and g == KV_HEADS - 1)

                def rotate_first(j):
                    times_cos(ng, nxt, j)
                    if refill:
                        split_attention(g + 1, j)

                if c == 0:
                    for tile in range(O_TILE, W_TILES):
                        split_attention(g, tile)
                if has_next:
                    rotate_first(K_TILE)
                masked_scores(g, c, 1)
                if not has_next:
                    add_output(g, c - 1, 2)
                reciprocals(g, c, 0)
                if has_next:
                    add_sin(ng, nxt, K_TILE)
                    rotate_first(Q_TILE)
                    rotate_first(Q_TILE + 1)
                reciprocals(g, c, 1)
                if has_next:
                    add_sin(ng, nxt, Q_TILE)
                    rotate_first(Q_TILE + 2)
                pt_low(g, c, 0, 0)
                if has_next:
                    add_sin(ng, nxt, Q_TILE + 1)
                pt_low(g, c, 0, 1)
                part_low(g, c, 0)
                if not has_next:
                    add_output(g, c - 1, 3)
                if has_next:
                    rotate_first(Q_TILE + 3)
                at_low(g, c, 0, 0)
                if has_next:
                    add_sin(ng, nxt, Q_TILE + 2)
                    add_sin(ng, nxt, Q_TILE + 3)
                pt_low(g, c, 1, 0)
                at_low(g, c, 0, 1)
                pt_low(g, c, 1, 1)
                part_low(g, c, 1)
                add_output(g, c, 0)
                at_low(g, c, 1, 0)
                add_output(g, c, 1)
                if not puts_off(g, c):
                    add_output(g, c, 2)
                at_low(g, c, 1, 1)
                if has_next:
                    masked_scores(ng, nxt, 0)
                    v_low(ng, nxt)
                if refill:
                    split_attention(g + 1, V_TILE)
                if not puts_off(g, c):
                    add_output(g, c, 3)

            dve.wait_ge(tables_loaded, 48)
            for j in range(1 + G):
                times_cos(0, 0, j)
                if j < IN_TILES - 4:
                    split_first(4 + j)
                s = swap[:, j % 2, :]
                sin = rope_sb[:, 1:2, :].broadcast_to([P, CHUNK // SEQ, SEQ])
                nc.vector.tensor_tensor(halves(s), halves(s), sin, ALU.mult).then_inc(sin_done, 1)
                add_sin(0, 0, j)
            masked_scores(0, 0, 0)
            v_low(0, 0)
            with dve.Fori(0, KV_HEADS - 1) as g:
                for c in range(CHUNKS):
                    step(g, c, True)
            for c in range(CHUNKS):
                step(KV_HEADS - 1, c, c < CHUNKS - 1)

        @block.gpsimd
        def _(pool):
            nc.gpsimd.memset(power[:], -0.5).then_inc(power_set, 1)
            pool.wait_ge(power_set, 1)
            for c in range(CHUNKS):
                cols = slice(c * TB, (c + 1) * TB)
                pool.wait_ge(eps_added, c + 1)
                nc.gpsimd.tensor_tensor(rstd[:, cols], var_eps[:, cols], power[:],
                                        ALU.pow).then_inc(rstd_done, 1)

            def spread_peak(which, count):
                found = held(pool, count)
                pool.wait_ge(peak_done, 1)
                pool.wait_ge(peak_done, found)
                nc.gpsimd.partition_all_reduce(flags[:, which:which + 1], peaks[:, which:which + 1], P,
                                               bass.bass_isa.ReduceOp.max).then_inc(flag_done, 1)

            def ff_pass(r, has_next, first=False):
                for n in range(GU):
                    if first and n == 2:
                        spread_peak(GATE_UP, 1)
                    if n == CHUNKS + 2:
                        spread_peak(DOWN, in_pass(r, 2, 1))
                    pool.wait_ge(h_hi_done, in_pass(r, GU, n))
                    cols = (slice(None), n // CHUNKS, tokens(n % CHUNKS))
                    nc.gpsimd.tensor_tensor(h_lo[cols], h32[:, n % 2, :], f32(h_hi[cols]),
                                            ALU.subtract).then_inc(h_lo_done, 1)
                for m in range(TILES):
                    if m == 4 and has_next:
                        spread_peak(GATE_UP, in_pass(r + 1, 2, 0))
                    pool.wait_ge(down_scaled, in_pass(r, TILES, m, TILES))
                    pool.wait_ge(ff_added, in_pass(r, TILES, m - TILES, TILES))
                    nc.gpsimd.tensor_tensor(acc[:, m, :], acc[:, m, :], scaled[:, m % SCALED, :],
                                            ALU.add).then_inc(ff_added, 1)

            pool.wait_ge(xn_done, TILES)
            ff_pass(0, True, first=True)
            with pool.Fori(1, PAIRS - 1) as r:
                ff_pass(r, True)
            ff_pass(PAIRS - 1, False)

            def split_attention(g, tile):
                pool.wait_ge(aw_hi_done, g * W_TILES + (tile + 1))
                nc.gpsimd.tensor_tensor(aw_lo[:, tile, :], araw[:, tile % RAW, :], f32(aw_hi[:, tile, :]),
                                        ALU.subtract).then_inc(aw_lo_done, 1)

            def times_sin(g, c, j):
                n = (1 + G) * c + j
                pool.wait_ge(swapped, in_step(g, c, 1 + G, j))
                s = swap[:, n % 2, :].rearrange("p (b s) -> p b s", s=SEQ)
                sin = rope_sb[:, 1:2, :].broadcast_to([P, CHUNK // SEQ, SEQ])
                nc.gpsimd.tensor_tensor(s, s, sin, ALU.mult).then_inc(sin_done, 1)

            def normalise(g, c, b):
                pool.wait_ge(rsums_done, in_step(g, c, 2, b))

                def r(cols):
                    return rsums[:, b, cols].unsqueeze(2).broadcast_to([P, G, P])

                early, late = s_early[:, b, :, :], s_late[:, b, :, 0:P]
                nc.gpsimd.tensor_tensor(early, early, r(slice(G, 2 * G)), ALU.mult).then_inc(probs_done, 1)
                nc.gpsimd.tensor_tensor(late, late, s_late[:, b, :, P:2 * P], ALU.add).then_inc(late_merged, 1)
                pool.wait_ge(late_merged, in_step(g, c, 2, b))
                nc.gpsimd.tensor_tensor(late, late, r(slice(0, G)), ALU.mult).then_inc(probs_done, 1)

            def part_high(g, c, b):
                pool.wait_ge(pt_hi_done, in_step(g, c, 4, 2 * b + 1))
                pool.wait_ge(pt_done, in_step(g, c, 4, 2 * b + 1, 4))
                early_keys, late_keys = parted(pt_hi)
                nc.gpsimd.tensor_tensor(late_keys, f32(early_keys), side(1), ALU.mult)
                nc.gpsimd.tensor_tensor(early_keys, f32(early_keys), side(0), ALU.mult).then_inc(hi_parted, 1)

            def step(g, c, has_next):
                ng, nxt = (g, c + 1) if c + 1 < CHUNKS else (g + 1, 0)
                refill = c == CHUNKS - 2 and not (isinstance(g, int) and g == KV_HEADS - 1)
                if c == 0:
                    for tile in range(O_TILE, W_TILES):
                        split_attention(g, tile)
                if has_next:
                    times_sin(ng, nxt, K_TILE)
                normalise(g, c, 0)
                if refill:
                    split_attention(g + 1, K_TILE)
                if has_next:
                    times_sin(ng, nxt, Q_TILE)
                    times_sin(ng, nxt, Q_TILE + 1)
                normalise(g, c, 1)
                part_high(g, c, 0)
                if has_next:
                    times_sin(ng, nxt, Q_TILE + 2)
                    times_sin(ng, nxt, Q_TILE + 3)
                part_high(g, c, 1)
                if refill:
                    for tile in range(Q_TILE, IN_TILES):
                        split_attention(g + 1, tile)

            pool.wait_ge(tables_loaded, 48)
            with pool.Fori(0, KV_HEADS - 1) as g:
                for c in range(CHUNKS):
                    step(g, c, True)
            for c in range(CHUNKS):
                step(KV_HEADS - 1, c, c < CHUNKS - 1)


def kernel(L0_attn_x, L0_attn_wq, L0_attn_wk, L0_attn_wv, L0_attn_wo, L0_ffn_gate_t, L0_ffn_up_t,
           L0_ffn_down_t, L0_ffn_gate_s, L0_ffn_up_s, L0_ffn_down_s):
    import concourse.bacc as bacc
    from concourse.bass_utils import run_bass_kernel_spmd

    def columns(w, blocks):
        w = np.asarray(w).reshape(KB, P, blocks, P)
        return np.ascontiguousarray(w.transpose(2, 1, 0, 3)).reshape(blocks, P, KB * P)

    def rows(w):
        return np.ascontiguousarray(w).reshape(-1, P, HID)

    data = {
        "x": np.asarray(L0_attn_x).reshape(TOKENS, HID),
        "wq": columns(L0_attn_wq, Q_HEADS),
        "wk": columns(L0_attn_wk, KV_HEADS),
        "wv": columns(L0_attn_wv, KV_HEADS),
        "wo": rows(np.asarray(L0_attn_wo)),
        "gate": columns(np.asarray(L0_ffn_gate_t).T, FBLOCKS),
        "up": columns(np.asarray(L0_ffn_up_t).T, FBLOCKS),
        "down": rows(np.asarray(L0_ffn_down_t).T),
        "gate_s": np.ascontiguousarray(np.asarray(L0_ffn_gate_s).reshape(FBLOCKS, P).T),
        "up_s": np.ascontiguousarray(np.asarray(L0_ffn_up_s).reshape(FBLOCKS, P).T),
        "down_s": np.asarray(L0_ffn_down_s),
        "rope": rope_tables(),
        "masks": score_masks(),
        "sides": key_sides(),
        "ident": np.eye(P, dtype=np.float32),
    }
    nc = bacc.Bacc("TRN2", target_bir_lowering=False, num_devices=1)
    aps = [nc.dram_tensor(n, a.shape, mybir.dt.from_np(a.dtype), kind="ExternalInput").ap()
           for n, a in data.items()]
    out = nc.dram_tensor("out", (TOKENS, HID), F32, kind="ExternalOutput").ap()
    block_kernel(nc, *aps, out)
    result = run_bass_kernel_spmd(nc, [data], core_ids=[0])
    return result.results[0]["out"].reshape(BATCH, SEQ, HID)
```

```python
from contextlib import ExitStack

import concourse.bass as bass
import numpy as np
from concourse import mybir

F32 = mybir.dt.float32
F32R = mybir.dt.float32r
I32 = mybir.dt.int32
BF16 = mybir.dt.bfloat16
ACT = mybir.ActivationFunctionType
ALU = mybir.AluOpType
AX = mybir.AxisListType

P = 128
BATCH, SEQ, HID = 8, 256, 512
TOKENS = BATCH * SEQ
FF = 1792
Q_HEADS, KV_HEADS, DH = 32, 8, 128
HALF = DH // 2
WINDOW = 128
THETA = 10000.0
EPS = 1e-5
SM_SCALE = DH ** -0.5
MASKED = -3.0e38
BIGGEST = 3.4e38

KB = HID // P
CHUNK = 512
CHUNKS = TOKENS // CHUNK
TB = CHUNK // P
G = Q_HEADS // KV_HEADS
FBLOCKS = FF // P
PAIRS = FBLOCKS // 2
TILES = TOKENS // P

K_TILE, Q_TILE, V_TILE, O_TILE = 0, 1, 1 + G, 2 + G
IN_TILES, W_TILES = 2 + G, 2 + 2 * G
RAW = 4
BATCHES = [range(t, t + TB // 2) for t in range(0, TILES, TB // 2)]
BY_DVE = 2
F_TILES = 6


def rope_tables():
    inv_freq = np.float32(THETA) ** (-np.arange(HALF, dtype=np.float32) / np.float32(HALF))
    angle = np.arange(SEQ, dtype=np.float32)[None, :] * inv_freq.astype(np.float32)[:, None]
    cos, sin = np.cos(angle), np.sin(angle)
    return np.concatenate([np.concatenate([cos, cos]), np.concatenate([-sin, sin])], axis=1).astype(np.float32)


def score_masks():
    i, j = np.arange(P)[:, None], np.arange(P)[None, :]
    causal = np.where(j <= i, 0.0, MASKED)
    window = np.where(j > i + P - WINDOW, 0.0, MASKED)
    return np.concatenate([causal, window, causal], axis=1).astype(np.float32)


def key_sides():
    j, i = np.arange(P)[:, None], np.arange(P)[None, :]
    return np.concatenate([j > i, j <= i], axis=1).astype(np.float32)


def block_kernel(nc, x, wq, wk, wv, wo, gate, up, down, gate_s, up_s, down_s, rope, masks, sides, ident, out):
    with ExitStack() as ctx:
        def sem(name):
            return ctx.enter_context(nc.semaphore(name))

        def tensors(stack, **shapes):
            return [stack.enter_context(nc.sbuf_tensor(n, s, d)) for n, (s, d) in shapes.items()]

        xt_hi, xt_lo, acc, rope_sb, mask_sb, side_sb, ident_sb = tensors(
            ctx, xt_hi=([P, KB, TOKENS], F32R), xt_lo=([P, KB, TOKENS], F32R),
            acc=([P, TILES, HID], F32), rope_sb=([P, 2, SEQ], F32), mask_sb=([P, 3 * P], F32),
            side_sb=([P, 2, P], F32), ident_sb=([P, P], F32))
        with ExitStack() as ff:
            (gu_hi, d_hi, d_lo, magnitudes, gu_lo, h_hi, h_lo, fraw, gs_sb, us_sb, ds_sb, stats, moments,
             var_eps, power, rstd, peaks, flags, xn, gated, h32) = tensors(
                ff, gu_hi=([P, 4, 512], F32R), d_hi=([P, 2, 512], F32R), d_lo=([P, 2, 512], F32R),
                magnitudes=([P, 4, 512], BF16), gu_lo=([P, 4, 512], F32R),
                h_hi=([P, 2, TOKENS], F32R), h_lo=([P, 2, TOKENS], F32R),
                fraw=([P, F_TILES, 512], I32),
                gs_sb=([P, FBLOCKS], F32), us_sb=([P, FBLOCKS], F32), ds_sb=([P, HID], F32),
                stats=([P, TILES, 6], F32), moments=([P, TILES, 2], F32), var_eps=([P, TILES], F32), power=([P, TB], F32),
                rstd=([P, TILES], F32), peaks=([P, 2], F32), flags=([P, 2], F32),
                xn=([P, 2, TB, HID], F32), gated=([P, 2, CHUNK], F32), h32=([P, 2, CHUNK], F32))
        with ExitStack() as same_place:
            _, _, q_lo_space = tensors(
                same_place, above_hi=([P, W_TILES, 512], F32R), above_lo=([P, W_TILES, 512], F32R),
                q_lo_space=([P, G, CHUNK], F32R))
        (aw_hi, aw_lo, q_sb, q_hi, k_sb, k_hi, k_lo, swap, v_hi, v_lo, s_late, s_early, pt_hi, pt_lo,
         at_hi, at_lo, negmax, sums, rsums, araw) = tensors(
            ctx, aw_hi=([P, W_TILES, 512], F32R), aw_lo=([P, W_TILES, 512], F32R),
            q_sb=([P, G, CHUNK], F32), q_hi=([P, G, TB // 2, P], F32R),
            k_sb=([P, CHUNK], F32), k_hi=([P, CHUNK], F32R), k_lo=([P, CHUNK], F32R),
            swap=([P, 2, CHUNK], F32), v_hi=([P, TB, DH], F32R), v_lo=([P, TB, DH], F32R),
            s_late=([P, 2, G, 2 * P], F32), s_early=([P, 2, G, P], F32),
            pt_hi=([P, 3, G * P], F32R), pt_lo=([P, 3, G * P], F32R),
            at_hi=([P, 2, G * P], F32R), at_lo=([P, 2, G * P], F32R),
            negmax=([P, 2, 2 * G], F32), sums=([P, 2, 2 * G], F32), rsums=([P, 2, 2 * G], F32),
            araw=([P, RAW, 512], F32))
        scaled = xn[:].rearrange("p a t h -> p (a t) h")
        SCALED = 2 * TB
        vt_sb = swap[:, 1, :]
        q_late, q_lo = [q[:].rearrange("p h (b s) -> p h b s", s=SEQ)[:, :, :, P:SEQ]
                        for q in (q_sb, q_lo_space)]
        bank = [ctx.enter_context(nc.psum_tensor(f"bank{i}", [P, 512], F32)) for i in range(8)]

        x_loaded = [[sem(f"x_loaded{c}_{t}") for t in range(TB)] for c in range(CHUNKS)]
        ident_loaded, scales_loaded, tables_loaded = sem("ident_loaded"), sem("scales_loaded"), sem("tables_loaded")
        stats_done, moments_done, eps_added = sem("stats_done"), sem("moments_done"), sem("eps_added")
        power_set, rstd_done, xn_done = sem("power_set"), sem("rstd_done"), sem("xn_done")
        xt_ready, xt_hi_done, xt_lo_done = sem("xt_ready"), sem("xt_hi_done"), sem("xt_lo_done")
        fraw_loaded = [sem(f"fraw_loaded{i}") for i in range(F_TILES)]
        fw_hi_done, fw_lo_done = sem("fw_hi_done"), sem("fw_lo_done")
        peak_done, flag_done = sem("peak_done"), sem("flag_done")
        gate_ready, up_ready, silu_done, h32_done = sem("gate_ready"), sem("up_ready"), sem("silu_done"), sem("h32_done")
        h_hi_done, h_lo_done = sem("h_hi_done"), sem("h_lo_done")
        down_ready, down_scaled, ff_added = sem("down_ready"), sem("down_scaled"), sem("ff_added")
        araw_loaded = [sem(f"araw_loaded{i}") for i in range(RAW)]
        aw_hi_done, aw_lo_done, last_aw_lo_done = (
            sem("aw_hi_done"), sem("aw_lo_done"), sem("last_aw_lo_done"))
        proj_ready, swapped, cos_done, sin_done, qk_done = (
            sem("proj_ready"), sem("swapped"), sem("cos_done"), sem("sin_done"), sem("qk_done"))
        qk_hi_done, qk_lo_done = sem("qk_hi_done"), sem("qk_lo_done")
        vt_done, v_ready, v_hi_done, v_done = sem("vt_done"), sem("v_ready"), sem("v_hi_done"), sem("v_done")
        scores_ready, scores_used, exp_done = sem("scores_ready"), sem("scores_used"), sem("exp_done")
        rsums_done, probs_done = sem("rsums_done"), sem("probs_done")
        late_merged, pt_ready, pt_hi_done, pt_done = (
            sem("late_merged"), sem("pt_ready"), sem("pt_hi_done"), sem("pt_done"))
        hi_parted, lo_parted = sem("hi_parted"), sem("lo_parted")
        at_ready, at_hi_done, at_done = sem("at_ready"), sem("at_hi_done"), sem("at_done")
        wo_ready, wo_added, stored = sem("wo_ready"), sem("wo_added"), sem("stored")

        def in_pass(r, per_pass, item, before=0):
            return r * per_pass + (item + 1 + before)

        def in_step(g, c, per_step, item, before=0):
            return g * (CHUNKS * per_step) + (c * per_step + item + 1 + before)

        def puts_off(g, c):
            return isinstance(g, int) and (g, c) == (KV_HEADS - 1, CHUNKS - 2)

        def held(engine, count):
            return count if isinstance(count, int) else engine.to_reg(count)

        def tokens(c):
            return slice(c * CHUNK, (c + 1) * CHUNK)

        def f32(ap):
            return ap.bitcast(F32)

        def part(engine, pt):
            early_keys, late_keys = [pt[:, i, :].rearrange("p (h i) -> p h i", h=G) for i in (1, 2)]
            is_early, is_late = [side_sb[:, i:i + 1, :].broadcast_to([P, G, P]) for i in (0, 1)]
            engine.tensor_tensor(late_keys, f32(early_keys), is_late, ALU.mult)
            return engine.tensor_tensor(early_keys, f32(early_keys), is_early, ALU.mult)

        def weight_block(w, tile, kb):
            return w[:, tile, kb * P:(kb + 1) * P]

        def fw_hi(tile):
            return gu_hi[:, tile, :] if tile < 4 else d_hi[:, tile - 4, :]

        def fw_lo(tile):
            return gu_lo[:, tile, :] if tile < 4 else d_lo[:, tile - 4, :]

        def tiles_of_slot(slot):
            return len(range(slot, W_TILES, RAW))

        def tile_is_split(engine, g, tile):
            if tile < W_TILES - BY_DVE:
                engine.wait_ge(aw_lo_done, g * (W_TILES - BY_DVE) + (tile + 1))
            else:
                engine.wait_ge(last_aw_lo_done, g * BY_DVE + (tile - (W_TILES - BY_DVE) + 1))

        GU = 2 * CHUNKS
        GATE_UP, DOWN = 0, 1
        PT_BANK = (5, 6)
        AT_BANK = 7

        block = ctx.enter_context(nc.Block())

        @block.sync
        def _(sp):
            x_v = x.rearrange("(c t p) h -> c p t h", c=CHUNKS, p=P)
            out_v = out.rearrange("(c t p) h -> c p t h", c=CHUNKS, p=P)
            def load_x(c):
                for t in range(TB):
                    sp.dma_start(acc[:, c * TB + t, :], x_v[c][:, t, :]).then_inc(x_loaded[c][t], 16)

            def load_ff(r, tile):
                src = (gate, up, gate, up, down, down)[tile]
                f = r * 2 + (0, 0, 1, 1, 0, 1)[tile]
                sp.dma_start(fraw[:, tile, :], src[f]).then_inc(fraw_loaded[tile], 16)

            load_x(0)
            sp.dma_start(ident_sb[:], ident).then_inc(ident_loaded, 16)
            for tile in (0, 1):
                load_ff(0, tile)
            load_x(1)
            for dst, src in ((gs_sb, gate_s), (us_sb, up_s)):
                sp.dma_start(dst[:], src).then_inc(scales_loaded, 16)
            sp.dma_start(ds_sb[:], down_s.partition_broadcast(P)).then_inc(scales_loaded, 16)
            load_x(2)
            for tile in (2, 3):
                load_ff(0, tile)
            load_x(3)
            for tile in (4, 5):
                load_ff(0, tile)
            sp.dma_start(rope_sb[:].rearrange("p a s -> p (a s)"), rope).then_inc(tables_loaded, 16)
            sp.dma_start(mask_sb[:], masks).then_inc(tables_loaded, 16)
            sp.dma_start(side_sb[:].rearrange("p a i -> p (a i)"), sides).then_inc(tables_loaded, 16)
            with sp.Fori(0, PAIRS - 1) as r:
                for tile in range(F_TILES):
                    sp.wait_ge(fw_lo_done, in_pass(r, F_TILES, tile))
                    load_ff(r + 1, tile)

            def load_attention(g, tile):
                slot = tile % RAW
                if tile == K_TILE:
                    src = wk[g]
                elif tile < V_TILE:
                    src = wq[g * G + (tile - Q_TILE)]
                elif tile == V_TILE:
                    src = wv[g]
                else:
                    src = wo[g * G + (tile - O_TILE)]
                sp.dma_start(araw[:, slot, :], src).then_inc(araw_loaded[slot], 16)

            sp.wait_ge(h_lo_done, GU * (PAIRS + 1))
            for tile in range(RAW):
                load_attention(0, tile)
            for tile in range(RAW, W_TILES):
                tile_is_split(sp, 0, tile - RAW)
                load_attention(0, tile)
            with sp.Fori(0, KV_HEADS - 1) as g:
                for tile in range(W_TILES):
                    if tile >= RAW:
                        tile_is_split(sp, g + 1, tile - RAW)
                    else:
                        tile_is_split(sp, g, tile + RAW * (tiles_of_slot(tile) - 1))
                    load_attention(g + 1, tile)

            for c in range(CHUNKS):
                for t in range(TB):
                    sp.wait_ge(wo_added, in_step(KV_HEADS - 1, c, TB, t, TB))
                    sp.dma_start(out_v[c][:, t, :], acc[:, c * TB + t, :]).then_inc(stored, 16)
            sp.wait_ge(stored, 16 * TILES)

        @block.tensor
        def _(pe):
            def product(dst, w_hi, w_lo, x_hi, x_lo, first, last, w_lo_too=True, x_lo_too=True):
                passes = [(w_hi, x_hi)] + [(w_hi, x_lo)] * x_lo_too + [(w_lo, x_hi)] * w_lo_too
                for n, (w, v) in enumerate(passes):
                    mm = nc.tensor.matmul(dst, w, v, start=first and n == 0,
                                          stop=last and n == len(passes) - 1)
                return mm

            def transpose_rows(c):
                def transpose_block(kb, t):
                    return nc.tensor.transpose(bank[4 + kb][:, t * P:(t + 1) * P],
                                               xn[:, c % 2, t, kb * P:(kb + 1) * P], ident_sb[:])

                if c == 0:
                    for t in range(TB):
                        pe.wait_ge(xn_done, t + 1)
                        for kb in range(KB):
                            last = transpose_block(kb, t)
                            if t == TB - 1:
                                last.then_inc(xt_ready, 1)
                    return
                pe.wait_ge(xn_done, TB * (c + 1))
                for kb in range(KB):
                    pe.wait_ge(xt_lo_done, (c - 1) * KB + kb + 1)
                    for t in range(TB):
                        last = transpose_block(kb, t)
                    last.then_inc(xt_ready, 1)

            def gate_or_up(r, f, c, which, with_lo):
                n = f * CHUNKS + c
                ready, free = ((gate_ready, silu_done), (up_ready, h32_done))[which]
                if c == 0:
                    pe.wait_ge(fw_lo_done, in_pass(r, F_TILES, 2 * f + which))
                pe.wait_ge(free, in_pass(r, GU, n - 2, GU))
                for kb in range(KB):
                    if isinstance(r, int) and (f, which) == (0, 0):
                        pe.wait_ge(xt_lo_done, KB * c + kb + 1)
                    last = product(bank[2 * which + n % 2][:], weight_block(gu_hi, 2 * f + which, kb),
                                   weight_block(gu_lo, 2 * f + which, kb), xt_hi[:, kb, tokens(c)],
                                   xt_lo[:, kb, tokens(c)], kb == 0, kb == KB - 1, w_lo_too=with_lo)
                last.then_inc(ready, 1)

            def gates_and_ups(r, blocks, with_lo):
                for f in blocks:
                    for c in range(CHUNKS):
                        for which in range(2):
                            gate_or_up(r, f, c, which, with_lo)

            def downs(r, with_lo):
                for m in range(TILES):
                    c = m // TB
                    if m % TB == 0:
                        pe.wait_ge(h_lo_done, in_pass(r, GU, CHUNKS + c, GU))
                    pe.wait_ge(down_scaled, in_pass(r, TILES, m - 4, TILES))
                    rows = slice(m * P, (m + 1) * P)
                    for f in range(2):
                        last = product(bank[4 + m % 4][:], h_hi[:, f, rows], h_lo[:, f, rows],
                                       d_hi[:, f, :], d_lo[:, f, :], f == 0, f == 1,
                                       x_lo_too=with_lo)
                    last.then_inc(down_ready, 1)

            def by_flag(r, which, work):
                known = held(pe, in_pass(r, 2, 0 if which == GATE_UP else 1))
                pe.wait_ge(flag_done, 1)
                pe.wait_ge(flag_done, known)
                biggest_lo = pe.value_load(flags[0:1, which:which + 1].bitcast(I32))
                with pe.If_ne(pe.to_reg(biggest_lo), 0):
                    work(True)
                with pe.Else():
                    work(False)

            def ff_pass(r, blocks):
                by_flag(r, GATE_UP, lambda with_lo: gates_and_ups(r, blocks, with_lo))
                by_flag(r, DOWN, lambda with_lo: downs(r, with_lo))

            pe.wait_ge(ident_loaded, 16)
            transpose_rows(0)
            for c in range(CHUNKS):
                gate_or_up(0, 0, c, 0, True)
                gate_or_up(0, 0, c, 1, True)
                if c + 1 < CHUNKS:
                    transpose_rows(c + 1)
            ff_pass(0, (1,))
            with pe.Fori(1, PAIRS) as r:
                ff_pass(r, (0, 1))

            def project(g, c, j):
                if c == 0:
                    tile_is_split(pe, g, j)
                if j >= 2:
                    pe.wait_ge(cos_done, in_step(g, c, 1 + G, j - 2))
                for kb in range(KB):
                    last = product(bank[j % 2][:], weight_block(aw_hi, j, kb), weight_block(aw_lo, j, kb),
                                   xt_hi[:, kb, tokens(c)], xt_lo[:, kb, tokens(c)], kb == 0, kb == KB - 1)
                last.then_inc(proj_ready, 1)

            def project_next(g, c, j):
                if j < 2:
                    pe.wait_ge(wo_added, in_step(g, c - 1, TB, 2 + j, TB))
                if c + 1 < CHUNKS:
                    project(g, c + 1, j)
                else:
                    project(g + 1, 0, j)

            def transpose_v():
                for t in range(TB):
                    last = nc.tensor.transpose(bank[AT_BANK][:, t * DH:(t + 1) * DH],
                                               vt_sb[:, t * P:(t + 1) * P], ident_sb[:])
                last.then_inc(v_ready, 1)

            def scores(g, c, b):
                early, keys = b * SEQ, slice(b * SEQ, (b + 1) * SEQ)
                for pair in range(G // 2):
                    if b == 0:
                        pe.wait_ge(qk_lo_done, in_step(g, c, 1 + G // 2, 1 + pair))
                    pe.wait_ge(scores_used, in_step(g, c, 6, 3 * b + pair - 3, 6))
                    for h in (2 * pair, 2 * pair + 1):
                        last = product(bank[2 + pair][:, (h % 2) * SEQ:(h % 2 + 1) * SEQ], q_hi[:, h, b, :],
                                       q_lo[:, h, b, :], k_hi[:, keys], k_lo[:, keys], True, True)
                    last.then_inc(scores_ready, 1)
                if b == 0:
                    pe.wait_ge(qk_done, in_step(g, c, 1 + G, G))
                pe.wait_ge(scores_used, in_step(g, c, 6, 3 * b - 1, 6))
                for h in range(G):
                    last = nc.tensor.matmul(bank[4][:, h * P:(h + 1) * P], q_sb[:, h, early:early + P],
                                            k_sb[:, early:early + P], start=True, stop=True)
                last.then_inc(scores_ready, 1)

            def transpose_probs(g, c, b, late):
                n = 2 * b + late
                pe.wait_ge(probs_done, in_step(g, c, 4, n))
                pe.wait_ge(pt_done, in_step(g, c, 4, n - 2, 4))
                for h in range(G):
                    src = s_late[:, b, h, 0:P] if late else s_early[:, b, h, :]
                    last = nc.tensor.transpose(bank[PT_BANK[late]][:, h * P:(h + 1) * P], src, ident_sb[:])
                last.then_inc(pt_ready, 1)

            def attend(g, c, b, late):
                n = 2 * b + late
                if late:
                    pe.wait_ge(hi_parted, in_step(g, c, 2, b))
                    pe.wait_ge(lo_parted, in_step(g, c, 2, b))
                else:
                    pe.wait_ge(pt_done, in_step(g, c, 4, n, 4))
                if n == 0:
                    pe.wait_ge(v_done, in_step(g, c, 1, 0))
                else:
                    pe.wait_ge(at_done, in_step(g, c, 4, n - 1))
                tiles = ((1, 2 * b), (2, 2 * b + 1)) if late else ((0, 2 * b),)
                for k, (i, t) in enumerate(tiles):
                    last = product(bank[AT_BANK][:], v_hi[:, t, :], v_lo[:, t, :], pt_hi[:, i, :],
                                   pt_lo[:, i, :], k == 0, k == len(tiles) - 1)
                last.then_inc(at_ready, 1)

            def output(g, c, b, late, has_next):
                n = 2 * b + late
                pe.wait_ge(at_done, in_step(g, c, 4, n))
                if n == 0 and c == 0:
                    tile_is_split(pe, g, W_TILES - BY_DVE - 1)
                    tile_is_split(pe, g, W_TILES - 1)
                if n >= 2:
                    pe.wait_ge(wo_added, in_step(g, c, TB, n - 2, TB))
                elif not has_next:
                    pe.wait_ge(wo_added, in_step(g, c - 1, TB, n + 2, TB))
                elif n == 0:
                    pe.wait_ge(cos_done, in_step(g, c + 1, 1 + G, G))
                else:
                    pe.wait_ge(vt_done, in_step(g, c + 1, 1, 0))
                for h in range(G):
                    last = product(bank[n % 2][:], at_hi[:, late, h * P:(h + 1) * P],
                                   at_lo[:, late, h * P:(h + 1) * P], aw_hi[:, O_TILE + h, :],
                                   aw_lo[:, O_TILE + h, :], h == 0, h == G - 1)
                last.then_inc(wo_ready, 1)

            def step(g, c, has_next):
                ng, nxt = (g, c + 1) if c + 1 < CHUNKS else (g + 1, 0)
                scores(g, c, 1)
                if has_next:
                    for j in range(Q_TILE + G - 1):
                        project_next(g, c, j)
                else:
                    output(g, c - 1, 1, 0, True)
                    output(g, c - 1, 1, 1, True)
                transpose_probs(g, c, 0, 0)
                transpose_probs(g, c, 0, 1)
                if has_next:
                    project_next(g, c, Q_TILE + G - 1)
                attend(g, c, 0, 0)
                if has_next:
                    project_next(g, c, V_TILE)
                transpose_probs(g, c, 1, 0)
                if not has_next:
                    output(g, c, 0, 0, has_next)
                attend(g, c, 0, 1)
                transpose_probs(g, c, 1, 1)
                if has_next:
                    output(g, c, 0, 0, has_next)
                attend(g, c, 1, 0)
                output(g, c, 0, 1, has_next)
                if has_next and not puts_off(g, c):
                    output(g, c, 1, 0, has_next)
                attend(g, c, 1, 1)
                if not has_next:
                    output(g, c, 1, 0, has_next)
                if has_next:
                    scores(ng, nxt, 0)
                    pe.wait_ge(vt_done, in_step(g, c + 1, 1, 0))
                    pe.wait_ge(at_done, in_step(g, c, 4, 3))
                    transpose_v()
                if not puts_off(g, c):
                    output(g, c, 1, 1, has_next)

            for j in range(IN_TILES):
                project(0, 0, j)
            pe.wait_ge(vt_done, 1)
            pe.wait_ge(down_scaled, TILES * (PAIRS + 1))
            transpose_v()
            scores(0, 0, 0)
            with pe.Fori(0, KV_HEADS - 1) as g:
                for c in range(CHUNKS):
                    step(g, c, True)
            for c in range(CHUNKS):
                step(KV_HEADS - 1, c, c < CHUNKS - 1)

        @block.scalar
        def _(act):
            def xt_high(c):
                for kb in range(KB):
                    act.wait_ge(xt_ready, c * KB + kb + 1)
                    nc.scalar.activation(xt_hi[:, kb, tokens(c)], bank[4 + kb][:],
                                         ACT.Copy).then_inc(xt_hi_done, 1)

            def split_ff(r, tile):
                act.wait_ge(fraw_loaded[tile], r * 16 + 16)
                nc.scalar.activation(fw_hi(tile), fraw[:, tile, :], ACT.Copy).then_inc(fw_hi_done, 1)

            def h_high(r, n):
                act.wait_ge(h32_done, in_pass(r, GU, n, GU))
                nc.scalar.activation(h_hi[:, n // CHUNKS, tokens(n % CHUNKS)], h32[:, n % 2, :],
                                     ACT.Copy).then_inc(h_hi_done, 1)

            def find_peak(r, which):
                lo, last = (gu_lo, 3) if which == GATE_UP else (d_lo, 5)
                act.wait_ge(fw_lo_done, in_pass(r, F_TILES, last))
                nc.scalar.activation(magnitudes[:, 0:lo.shape[1], :], f32(lo[:]),
                                     ACT.Abs, accum_out=peaks[:, which:which + 1]).then_inc(peak_done, 1)

            def ff_pass(r, has_next, with_rows=False):
                for n in range(GU):
                    slot_read = held(act, in_pass(r, GU, n - 2, GU))
                    ready = held(act, in_pass(r, GU, n))
                    act.wait_ge(scales_loaded, 48)
                    act.wait_ge(gate_ready, ready)
                    act.wait_ge(h32_done, slot_read)
                    f = n // CHUNKS
                    nc.scalar.activation(gated[:, n % 2, :], bank[n % 2][:], ACT.Silu,
                                         scale=gs_sb[:, bass.ds(r * 2 + f, 1)]).then_inc(silu_done, 1)
                    if with_rows and n + 1 < CHUNKS:
                        xt_high(n + 1)
                    if n > 0:
                        h_high(r, n - 1)
                    if with_rows and n == CHUNKS - 2:
                        find_peak(0, GATE_UP)
                    if n == CHUNKS + 1:
                        find_peak(r, DOWN)
                    if with_rows and n == 0:
                        for tile in (2, 3):
                            split_ff(0, tile)
                    if n == (1 if with_rows else 0):
                        for tile in (4, 5):
                            split_ff(r, tile)
                    if n == CHUNKS and has_next:
                        act.wait_ge(up_ready, in_pass(r, GU, n - 1))
                        for tile in (0, 1):
                            split_ff(r + 1, tile)
                h_high(r, GU - 1)
                if has_next:
                    act.wait_ge(up_ready, in_pass(r, GU, GU - 1))
                    for tile in (2, 3):
                        split_ff(r + 1, tile)
                    find_peak(r + 1, GATE_UP)

            for tile in (0, 1):
                split_ff(0, tile)
            xt_high(0)
            ff_pass(0, True, with_rows=True)
            with act.Fori(1, PAIRS - 1) as r:
                ff_pass(r, True)
            ff_pass(PAIRS - 1, False)

            def swap_halves(g, c, j):
                act.wait_ge(proj_ready, in_step(g, c, IN_TILES, j))
                if j >= 2:
                    act.wait_ge(qk_done, in_step(g, c, 1 + G, j - 2))
                elif not (isinstance(g, int) and (g, c) == (0, 0)):
                    if j == 0:
                        act.wait_ge(qk_done, in_step(g, c, 1 + G, -1))
                    else:
                        act.wait_ge(v_ready, in_step(g, c, 1, -1))
                nc.scalar.activation(swap[0:HALF, j % 2, :], bank[j % 2][HALF:P, :], ACT.Copy)
                nc.scalar.activation(swap[HALF:P, j % 2, :], bank[j % 2][0:HALF, :],
                                     ACT.Copy).then_inc(swapped, 1)

            def copy_vt(g, c):
                act.wait_ge(proj_ready, in_step(g, c, IN_TILES, V_TILE))
                act.wait_ge(qk_done, in_step(g, c, 1 + G, V_TILE - 2))
                nc.scalar.activation(vt_sb, bank[V_TILE % 2][:], ACT.Copy).then_inc(vt_done, 1)

            def keys_high(g, c):
                act.wait_ge(qk_done, in_step(g, c, 1 + G, K_TILE))
                nc.scalar.activation(k_hi[:], k_sb[:], ACT.Copy).then_inc(qk_hi_done, 1)

            def queries_high(g, c, pair):
                act.wait_ge(qk_done, in_step(g, c, 1 + G, Q_TILE + 2 * pair + 1))
                for h in (2 * pair, 2 * pair + 1):
                    last = nc.scalar.activation(q_hi[:, h, :, :], q_late[:, h, :, :], ACT.Copy)
                last.then_inc(qk_hi_done, 1)

            def v_high(g, c):
                act.wait_ge(v_ready, in_step(g, c, 1, 0))
                nc.scalar.activation(v_hi[:].rearrange("p t d -> p (t d)"), bank[AT_BANK][:],
                                     ACT.Copy).then_inc(v_hi_done, 1)

            def exponentials(g, c, b, which):
                act.wait_ge(scores_used, in_step(g, c, 6, 3 * b + which, 6))
                heads = (0, 1, 2, 3) if which == 2 else (2 * which, 2 * which + 1)
                for h in heads:
                    s = s_early[:, b, h, :] if which == 2 else s_late[:, b, h, :]
                    col = h + (G if which == 2 else 0)
                    last = nc.scalar.activation(s, s, ACT.Exp, scale=-1.0, bias=negmax[:, b, col:col + 1],
                                                accum_out=sums[:, b, col:col + 1])
                last.then_inc(exp_done, 1)

            def pt_high(g, c, b, late):
                n = 2 * b + late
                act.wait_ge(pt_ready, in_step(g, c, 4, n))
                if b == 1:
                    act.wait_ge(at_ready, in_step(g, c, 4, late))
                nc.scalar.activation(pt_hi[:, late, :], bank[PT_BANK[late]][:],
                                     ACT.Copy).then_inc(pt_hi_done, 1)

            def at_high(g, c, b, late):
                n = 2 * b + late
                act.wait_ge(at_ready, in_step(g, c, 4, n))
                if b == 1:
                    act.wait_ge(wo_ready, in_step(g, c, TB, late))
                nc.scalar.activation(at_hi[:, late, :], bank[AT_BANK][:], ACT.Copy).then_inc(at_hi_done, 1)

            def step(g, c, has_next):
                ng, nxt = (g, c + 1) if c + 1 < CHUNKS else (g + 1, 0)
                for which in range(3):
                    exponentials(g, c, 0, which)
                exponentials(g, c, 1, 0)
                exponentials(g, c, 1, 1)
                if has_next:
                    swap_halves(ng, nxt, K_TILE)
                exponentials(g, c, 1, 2)
                if has_next:
                    swap_halves(ng, nxt, Q_TILE)
                    swap_halves(ng, nxt, Q_TILE + 1)
                    keys_high(ng, nxt)
                    swap_halves(ng, nxt, Q_TILE + 2)
                pt_high(g, c, 0, 0)
                pt_high(g, c, 0, 1)
                if has_next:
                    swap_halves(ng, nxt, Q_TILE + 3)
                at_high(g, c, 0, 0)
                if has_next:
                    queries_high(ng, nxt, 0)
                    copy_vt(ng, nxt)
                pt_high(g, c, 1, 0)
                if has_next:
                    queries_high(ng, nxt, 1)
                at_high(g, c, 0, 1)
                pt_high(g, c, 1, 1)
                at_high(g, c, 1, 0)
                at_high(g, c, 1, 1)
                if has_next:
                    v_high(ng, nxt)

            for j in range(1 + G):
                swap_halves(0, 0, j)
                if j == Q_TILE + 1:
                    keys_high(0, 0)
                if j == Q_TILE + 2:
                    queries_high(0, 0, 0)
            copy_vt(0, 0)
            queries_high(0, 0, 1)
            v_high(0, 0)
            with act.Fori(0, KV_HEADS - 1) as g:
                for c in range(CHUNKS):
                    step(g, c, True)
            for c in range(CHUNKS):
                step(KV_HEADS - 1, c, c < CHUNKS - 1)

        @block.vector
        def _(dve):
            for s, n in ((silu_done, GU), (h32_done, GU), (h_lo_done, GU), (down_scaled, TILES),
                         (ff_added, TILES), (scores_used, 6), (pt_done, 4), (wo_added, TB)):
                dve.sem_inc(s, n)

            def statistics(batch):
                tiles = BATCHES[batch]
                for tile in tiles:
                    dve.wait_ge(x_loaded[tile // TB][tile % TB], 16)
                    last = nc.vector.bn_stats(stats[:, tile, :], acc[:, tile, :])
                last.then_inc(stats_done, 1)
                dve.wait_ge(stats_done, batch + 1)
                for tile in tiles:
                    last = nc.vector.bn_aggr(moments[:, tile, :], stats[:, tile, :])
                last.then_inc(moments_done, 1)
                dve.wait_ge(moments_done, batch + 1)
                cols = slice(tiles.start, tiles.stop)
                nc.vector.tensor_scalar(var_eps[:, cols], moments[:, cols, 1], EPS, None,
                                        ALU.add).then_inc(eps_added, 1)

            def normalise(batch):
                dve.wait_ge(rstd_done, batch + 1)
                c = BATCHES[batch].start // TB
                if c >= 2:
                    dve.wait_ge(xt_ready, KB * (c - 1))
                for tile in BATCHES[batch]:
                    nc.vector.tensor_scalar(xn[:, c % 2, tile % TB, :], acc[:, tile, :],
                                            moments[:, tile, 0:1], rstd[:, tile:tile + 1], ALU.subtract,
                                            ALU.mult).then_inc(xn_done, 1)

            def xt_low(c):
                for kb in range(KB):
                    dve.wait_ge(xt_hi_done, c * KB + kb + 1)
                    nc.vector.tensor_tensor(xt_lo[:, kb, tokens(c)], bank[4 + kb][:],
                                            f32(xt_hi[:, kb, tokens(c)]),
                                            ALU.subtract).then_inc(xt_lo_done, 1)

            def hidden(r, n):
                dve.wait_ge(silu_done, in_pass(r, GU, n, GU))
                dve.wait_ge(up_ready, in_pass(r, GU, n))
                dve.wait_ge(h_lo_done, in_pass(r, GU, n - 2, GU))
                f = n // CHUNKS
                nc.vector.scalar_tensor_tensor(h32[:, n % 2, :], bank[2 + n % 2][:],
                                               us_sb[:, bass.ds(r * 2 + f, 1)], gated[:, n % 2, :],
                                               ALU.mult, ALU.mult).then_inc(h32_done, 1)

            def split_ff(r, tile):
                dve.wait_ge(fw_hi_done, in_pass(r, F_TILES, tile))
                nc.vector.tensor_tensor(fw_lo(tile), fraw[:, tile, :], f32(fw_hi(tile)),
                                        ALU.subtract).then_inc(fw_lo_done, 1)

            def split_attention(g, tile):
                slot = tile % RAW
                dve.wait_ge(araw_loaded[slot], g * (16 * tiles_of_slot(slot)) + (tile // RAW + 1) * 16)
                nc.vector.tensor_copy(aw_hi[:, tile, :], araw[:, slot, :]).then_inc(aw_hi_done, 1)

            def split_last(g):
                for tile in range(W_TILES - BY_DVE, W_TILES):
                    dve.wait_ge(aw_hi_done, g * W_TILES + (tile + 1))
                    nc.vector.tensor_tensor(aw_lo[:, tile, :], araw[:, tile % RAW, :], f32(aw_hi[:, tile, :]),
                                            ALU.subtract).then_inc(last_aw_lo_done, 1)

            def split_first(tile):
                split_attention(0, tile)
                dve.wait_ge(aw_hi_done, tile + 1)
                nc.vector.tensor_tensor(aw_lo[:, tile, :], araw[:, tile % RAW, :], f32(aw_hi[:, tile, :]),
                                        ALU.subtract).then_inc(aw_lo_done, 1)

            def ff_pass(r, has_next, with_rows=False):
                for n in range(GU):
                    if with_rows and n + 1 < CHUNKS:
                        if n + 2 < CHUNKS:
                            statistics(2 * (n + 2))
                        xt_low(n + 1)
                        if n + 2 < CHUNKS:
                            statistics(2 * (n + 2) + 1)
                            normalise(2 * (n + 2))
                            normalise(2 * (n + 2) + 1)
                    hidden(r, n)
                    if with_rows and n == 1:
                        for tile in (2, 3):
                            split_ff(0, tile)
                    if n == CHUNKS:
                        for tile in (4, 5):
                            split_ff(r, tile)
                    if n == CHUNKS + 1 and has_next:
                        for tile in (0, 1):
                            split_ff(r + 1, tile)
                for m in range(TILES):
                    if m == 2 and has_next:
                        for tile in (2, 3):
                            split_ff(r + 1, tile)
                    if m >= 8 and m % 2 == 0 and not has_next:
                        split_first(m // 2 - 4)
                    dve.wait_ge(down_ready, in_pass(r, TILES, m))
                    dve.wait_ge(ff_added, in_pass(r, TILES, m - SCALED, TILES))
                    nc.vector.tensor_tensor(scaled[:, m % SCALED, :], bank[4 + m % 4][:], ds_sb[:],
                                            ALU.mult).then_inc(down_scaled, 1)

            statistics(0)
            statistics(1)
            normalise(0)
            normalise(1)
            split_ff(0, 0)
            statistics(2)
            xt_low(0)
            split_ff(0, 1)
            statistics(3)
            normalise(2)
            normalise(3)
            dve.wait_ge(scales_loaded, 48)
            ff_pass(0, True, with_rows=True)
            with dve.Fori(1, PAIRS - 1) as r:
                ff_pass(r, True)
            ff_pass(PAIRS - 1, False)

            def rotated(dst_g, c, j):
                return k_sb[:] if j == K_TILE else q_sb[:, j - Q_TILE, :]

            def halves(ap):
                return ap.rearrange("p (b s) -> p b s", s=SEQ)

            def times_cos(g, c, j):
                dve.wait_ge(swapped, in_step(g, c, 1 + G, j))
                cos = rope_sb[:, 0:1, :].broadcast_to([P, CHUNK // SEQ, SEQ])
                nc.vector.tensor_tensor(halves(rotated(g, c, j)), halves(bank[j % 2][:]), cos,
                                        ALU.mult).then_inc(cos_done, 1)

            def add_sin(g, c, j):
                dve.wait_ge(sin_done, in_step(g, c, 1 + G, j))
                dve.wait_ge(cos_done, in_step(g, c, 1 + G, j))
                nc.vector.tensor_tensor(rotated(g, c, j), rotated(g, c, j), swap[:, j % 2, :],
                                        ALU.add).then_inc(qk_done, 1)

            def keys_low(g, c):
                dve.wait_ge(qk_hi_done, in_step(g, c, 1 + G // 2, 0))
                nc.vector.tensor_tensor(k_lo[:], k_sb[:], f32(k_hi[:]), ALU.subtract).then_inc(qk_lo_done, 1)

            def queries_low(g, c, pair):
                dve.wait_ge(qk_hi_done, in_step(g, c, 1 + G // 2, 1 + pair))
                for h in (2 * pair, 2 * pair + 1):
                    last = nc.vector.tensor_tensor(q_lo[:, h, :, :], q_late[:, h, :, :],
                                                   f32(q_hi[:, h, :, :]), ALU.subtract)
                last.then_inc(qk_lo_done, 1)

            def v_low(g, c):
                dve.wait_ge(v_hi_done, in_step(g, c, 1, 0))
                nc.vector.tensor_tensor(v_lo[:].rearrange("p t d -> p (t d)"), bank[AT_BANK][:],
                                        f32(v_hi[:]).rearrange("p t d -> p (t d)"),
                                        ALU.subtract).then_inc(v_done, 1)

            def masked_scores(g, c, b):
                for which in range(3):
                    ready = held(dve, in_step(g, c, 6, 3 * b + which))
                    dve.wait_ge(tables_loaded, 48)
                    dve.wait_ge(scores_ready, ready)
                    heads = (0, 1, 2, 3) if which == 2 else (2 * which, 2 * which + 1)
                    for h in heads:
                        if which == 2:
                            src, mask = bank[4][:, h * P:(h + 1) * P], mask_sb[:, 0:P]
                            dst, col = s_early[:, b, h, :], G + h
                        else:
                            src = bank[2 + which][:, (h % 2) * SEQ:(h % 2 + 1) * SEQ]
                            dst, col, mask = s_late[:, b, h, :], h, mask_sb[:, P:3 * P]
                        last = nc.vector.tensor_tensor_reduce(
                            out=dst, in0=src, in1=mask, scale=-SM_SCALE, scalar=BIGGEST, op0=ALU.add,
                            op1=ALU.min, accum_out=negmax[:, b, col:col + 1])
                    last.then_inc(scores_used, 1)

            def reciprocals(g, c, b):
                dve.wait_ge(exp_done, in_step(g, c, 6, 3 * b + 2))
                nc.vector.reciprocal(rsums[:, b, :], sums[:, b, :]).then_inc(rsums_done, 1)

            def pt_low(g, c, b, late):
                n = 2 * b + late
                dve.wait_ge(pt_hi_done, in_step(g, c, 4, n))
                nc.vector.tensor_tensor(pt_lo[:, late, :], bank[PT_BANK[late]][:], f32(pt_hi[:, late, :]),
                                        ALU.subtract).then_inc(pt_done, 1)

            def part_low(g, c, b):
                dve.wait_ge(pt_done, in_step(g, c, 4, 2 * b + 1, 4))
                part(nc.vector, pt_lo).then_inc(lo_parted, 1)

            def at_low(g, c, b, late):
                dve.wait_ge(at_hi_done, in_step(g, c, 4, 2 * b + late))
                nc.vector.tensor_tensor(at_lo[:, late, :], bank[AT_BANK][:], f32(at_hi[:, late, :]),
                                        ALU.subtract).then_inc(at_done, 1)

            def add_output(g, c, n):
                dve.wait_ge(wo_ready, in_step(g, c, TB, n))
                tile = c * TB + n
                nc.vector.tensor_tensor(acc[:, tile, :], bank[n % 2][:], acc[:, tile, :],
                                        ALU.add).then_inc(wo_added, 1)

            def step(g, c, has_next):
                ng, nxt = (g, c + 1) if c + 1 < CHUNKS else (g + 1, 0)
                refill = c == CHUNKS - 2 and not (isinstance(g, int) and g == KV_HEADS - 1)

                def rotate_first(j):
                    times_cos(ng, nxt, j)
                    if refill:
                        split_attention(g + 1, j)

                if c == 0:
                    for tile in range(O_TILE, W_TILES):
                        split_attention(g, tile)
                masked_scores(g, c, 1)
                reciprocals(g, c, 0)
                if c == 0:
                    split_last(g)
                if has_next:
                    rotate_first(K_TILE)
                if not has_next:
                    add_output(g, c - 1, 2)
                    add_output(g, c - 1, 3)
                if has_next:
                    rotate_first(Q_TILE)
                    add_sin(ng, nxt, K_TILE)
                reciprocals(g, c, 1)
                if has_next:
                    rotate_first(Q_TILE + 1)
                    add_sin(ng, nxt, Q_TILE)
                    rotate_first(Q_TILE + 2)
                pt_low(g, c, 0, 0)
                if has_next:
                    add_sin(ng, nxt, Q_TILE + 1)
                pt_low(g, c, 0, 1)
                part_low(g, c, 0)
                at_low(g, c, 0, 0)
                if not has_next:
                    part(nc.vector, pt_hi).then_inc(hi_parted, 1)
                if has_next:
                    times_cos(ng, nxt, Q_TILE + 3)
                    add_sin(ng, nxt, Q_TILE + 2)
                    keys_low(ng, nxt)
                    add_sin(ng, nxt, Q_TILE + 3)
                    queries_low(ng, nxt, 0)
                pt_low(g, c, 1, 0)
                at_low(g, c, 0, 1)
                pt_low(g, c, 1, 1)
                part_low(g, c, 1)
                if has_next:
                    queries_low(ng, nxt, 1)
                add_output(g, c, 0)
                at_low(g, c, 1, 0)
                add_output(g, c, 1)
                if has_next and not puts_off(g, c):
                    add_output(g, c, 2)
                at_low(g, c, 1, 1)
                if not has_next:
                    add_output(g, c, 2)
                if has_next:
                    masked_scores(ng, nxt, 0)
                    v_low(ng, nxt)
                if not puts_off(g, c):
                    add_output(g, c, 3)
                if refill:
                    split_attention(g + 1, Q_TILE + 3)
                    split_attention(g + 1, V_TILE)

            dve.wait_ge(tables_loaded, 48)
            for j in range(1 + G):
                times_cos(0, 0, j)
                if j < IN_TILES - 4:
                    split_first(4 + j)
                if j < 2:
                    s = swap[:, j, :]
                    sin = rope_sb[:, 1:2, :].broadcast_to([P, CHUNK // SEQ, SEQ])
                    nc.vector.tensor_tensor(halves(s), halves(s), sin, ALU.mult).then_inc(sin_done, 1)
                add_sin(0, 0, j)
                if j == Q_TILE + 1:
                    keys_low(0, 0)
                if j == Q_TILE + 2:
                    queries_low(0, 0, 0)
            queries_low(0, 0, 1)
            dve.wait_ge(ff_added, TILES * (PAIRS + 1))
            v_low(0, 0)
            masked_scores(0, 0, 0)
            with dve.Fori(0, KV_HEADS - 1) as g:
                for c in range(CHUNKS):
                    step(g, c, True)
            for c in range(CHUNKS):
                step(KV_HEADS - 1, c, c < CHUNKS - 1)

        @block.gpsimd
        def _(pool):
            nc.gpsimd.memset(power[:], -0.5).then_inc(power_set, 1)
            pool.wait_ge(power_set, 1)
            for batch, tiles in enumerate(BATCHES):
                cols = slice(tiles.start, tiles.stop)
                pool.wait_ge(eps_added, batch + 1)
                nc.gpsimd.tensor_tensor(rstd[:, cols], var_eps[:, cols], power[:, 0:len(tiles)],
                                        ALU.pow).then_inc(rstd_done, 1)

            def spread_peak(which, count):
                found = held(pool, count)
                pool.wait_ge(peak_done, 1)
                pool.wait_ge(peak_done, found)
                nc.gpsimd.partition_all_reduce(flags[:, which:which + 1], peaks[:, which:which + 1], P,
                                               bass.bass_isa.ReduceOp.max).then_inc(flag_done, 1)

            def ff_pass(r, has_next, first=False):
                for n in range(GU):
                    if first and n == 2:
                        spread_peak(GATE_UP, 1)
                    if n == CHUNKS + 2:
                        spread_peak(DOWN, in_pass(r, 2, 1))
                    pool.wait_ge(h_hi_done, in_pass(r, GU, n))
                    cols = (slice(None), n // CHUNKS, tokens(n % CHUNKS))
                    nc.gpsimd.tensor_tensor(h_lo[cols], h32[:, n % 2, :], f32(h_hi[cols]),
                                            ALU.subtract).then_inc(h_lo_done, 1)
                for m in range(TILES):
                    if m == 4 and has_next:
                        spread_peak(GATE_UP, in_pass(r + 1, 2, 0))
                    pool.wait_ge(down_scaled, in_pass(r, TILES, m, TILES))
                    pool.wait_ge(ff_added, in_pass(r, TILES, m - TILES, TILES))
                    nc.gpsimd.tensor_tensor(acc[:, m, :], acc[:, m, :], scaled[:, m % SCALED, :],
                                            ALU.add).then_inc(ff_added, 1)

            pool.wait_ge(xn_done, TILES)
            ff_pass(0, True, first=True)
            with pool.Fori(1, PAIRS - 1) as r:
                ff_pass(r, True)
            ff_pass(PAIRS - 1, False)

            def split_attention(g, tile):
                pool.wait_ge(aw_hi_done, g * W_TILES + (tile + 1))
                nc.gpsimd.tensor_tensor(aw_lo[:, tile, :], araw[:, tile % RAW, :], f32(aw_hi[:, tile, :]),
                                        ALU.subtract).then_inc(aw_lo_done, 1)

            def times_sin(g, c, j):
                pool.wait_ge(swapped, in_step(g, c, 1 + G, j))
                s = swap[:, j % 2, :].rearrange("p (b s) -> p b s", s=SEQ)
                sin = rope_sb[:, 1:2, :].broadcast_to([P, CHUNK // SEQ, SEQ])
                nc.gpsimd.tensor_tensor(s, s, sin, ALU.mult).then_inc(sin_done, 1)

            def normalise(g, c, b):
                pool.wait_ge(rsums_done, in_step(g, c, 2, b))

                def r(cols):
                    return rsums[:, b, cols].unsqueeze(2).broadcast_to([P, G, P])

                early, late = s_early[:, b, :, :], s_late[:, b, :, 0:P]
                nc.gpsimd.tensor_tensor(early, early, r(slice(G, 2 * G)), ALU.mult).then_inc(probs_done, 1)
                nc.gpsimd.tensor_tensor(late, late, s_late[:, b, :, P:2 * P], ALU.add).then_inc(late_merged, 1)
                pool.wait_ge(late_merged, in_step(g, c, 2, b))
                nc.gpsimd.tensor_tensor(late, late, r(slice(0, G)), ALU.mult).then_inc(probs_done, 1)

            def part_high(g, c, b):
                pool.wait_ge(pt_hi_done, in_step(g, c, 4, 2 * b + 1))
                pool.wait_ge(pt_done, in_step(g, c, 4, 2 * b + 1, 4))
                part(nc.gpsimd, pt_hi).then_inc(hi_parted, 1)

            def step(g, c, has_next):
                ng, nxt = (g, c + 1) if c + 1 < CHUNKS else (g + 1, 0)
                refill = c == CHUNKS - 2 and not (isinstance(g, int) and g == KV_HEADS - 1)
                if c == 0:
                    for tile in range(O_TILE, W_TILES - BY_DVE):
                        split_attention(g, tile)
                normalise(g, c, 0)
                if has_next:
                    times_sin(ng, nxt, K_TILE)
                    times_sin(ng, nxt, Q_TILE)
                normalise(g, c, 1)
                if has_next:
                    times_sin(ng, nxt, Q_TILE + 1)
                    times_sin(ng, nxt, Q_TILE + 2)
                    part_high(g, c, 0)
                    times_sin(ng, nxt, Q_TILE + 3)
                if refill:
                    split_attention(g + 1, K_TILE)
                    split_attention(g + 1, Q_TILE)
                part_high(g, c, 1)
                if refill:
                    for tile in range(Q_TILE + 1, IN_TILES):
                        split_attention(g + 1, tile)

            pool.wait_ge(tables_loaded, 48)
            pool.wait_ge(sin_done, 2)
            for j in range(2, 1 + G):
                times_sin(0, 0, j)
            with pool.Fori(0, KV_HEADS - 1) as g:
                for c in range(CHUNKS):
                    step(g, c, True)
            for c in range(CHUNKS):
                step(KV_HEADS - 1, c, c < CHUNKS - 1)


def kernel(L0_attn_x, L0_attn_wq, L0_attn_wk, L0_attn_wv, L0_attn_wo, L0_ffn_gate_t, L0_ffn_up_t,
           L0_ffn_down_t, L0_ffn_gate_s, L0_ffn_up_s, L0_ffn_down_s):
    import concourse.bacc as bacc
    from concourse.bass_utils import run_bass_kernel_spmd

    def columns(w, blocks):
        w = np.asarray(w).reshape(KB, P, blocks, P)
        return np.ascontiguousarray(w.transpose(2, 1, 0, 3)).reshape(blocks, P, KB * P)

    def rows(w):
        return np.ascontiguousarray(w).reshape(-1, P, HID)

    data = {
        "x": np.asarray(L0_attn_x).reshape(TOKENS, HID),
        "wq": columns(L0_attn_wq, Q_HEADS),
        "wk": columns(L0_attn_wk, KV_HEADS),
        "wv": columns(L0_attn_wv, KV_HEADS),
        "wo": rows(np.asarray(L0_attn_wo)),
        "gate": columns(np.asarray(L0_ffn_gate_t).T, FBLOCKS),
        "up": columns(np.asarray(L0_ffn_up_t).T, FBLOCKS),
        "down": rows(np.asarray(L0_ffn_down_t).T),
        "gate_s": np.ascontiguousarray(np.asarray(L0_ffn_gate_s).reshape(FBLOCKS, P).T),
        "up_s": np.ascontiguousarray(np.asarray(L0_ffn_up_s).reshape(FBLOCKS, P).T),
        "down_s": np.asarray(L0_ffn_down_s),
        "rope": rope_tables(),
        "masks": score_masks(),
        "sides": key_sides(),
        "ident": np.eye(P, dtype=np.float32),
    }
    nc = bacc.Bacc("TRN2", target_bir_lowering=False, num_devices=1)
    aps = [nc.dram_tensor(n, a.shape, mybir.dt.from_np(a.dtype), kind="ExternalInput").ap()
           for n, a in data.items()]
    out = nc.dram_tensor("out", (TOKENS, HID), F32, kind="ExternalOutput").ap()
    block_kernel(nc, *aps, out)
    result = run_bass_kernel_spmd(nc, [data], core_ids=[0])
    return result.results[0]["out"].reshape(BATCH, SEQ, HID)
```
